# Optimizing a Trainium2 kernel written in Bass

```python
import numpy as np
import jax
import jax.numpy as jnp

def _softmax(x, axis=-1):
    return jax.nn.softmax(x, axis=axis)

def _gelu(x):
    return jax.nn.gelu(x, approximate=True)

def _silu(x):
    return jax.nn.silu(x)

def _sigmoid(x):
    return jax.nn.sigmoid(x)

def _layernorm(x, axis=-1, eps=1e-05):
    m = jnp.mean(x, axis=axis, keepdims=True)
    v = jnp.var(x, axis=axis, keepdims=True)
    return (x - m) / jnp.sqrt(v + eps)

def _scatter_add(tgt, idx, src, axis=0):
    return tgt.at[idx].add(src)

def _segment_sum(src, seg, n):
    return jax.ops.segment_sum(src, seg, n)
kernel_name = 'mk_seq_preln_d1_jaxref_r8_72bc74'

def setup_inputs(seed: int=0):
    np.random.seed(seed)
    _w = jnp.asarray

    def _L0_attn_setup():
        import jax, jax.numpy as jnp
        import numpy as np
        import math
        HEAD_SIZE = 64

        def rotate_every_two(x):
            x1 = x[..., ::2]
            x2 = x[..., 1::2]
            return jnp.stack((-x2, x1), axis=-1).reshape(x.shape)

        def rope_table(seq_len, dtype=jnp.float32):
            pos = jnp.arange(seq_len, dtype=jnp.float32)
            inv = 10000.0 ** (jnp.arange(0, HEAD_SIZE, 2, dtype=jnp.float32) / HEAD_SIZE)
            radians = pos[:, None] / inv
            sincos = jnp.stack((jnp.sin(radians), jnp.cos(radians)), axis=-1).reshape(seq_len, -1)
            t = jnp.repeat(sincos, 2, axis=-1)
            return t.astype(dtype)
        key = jax.random.key(seed)
        ks = jax.random.split(key, 7)
        B, S, H = (2, 512, 128)
        sd = 1.0 / math.sqrt(H)
        return {'hidden_states': jax.random.normal(ks[0], (B, S, H), dtype=jnp.float32), 'Wq': jax.random.normal(ks[1], (H, H), dtype=jnp.float32) * sd, 'bq': jax.random.normal(ks[2], (H,), dtype=jnp.float32) * sd, 'Wk': jax.random.normal(ks[3], (H, H), dtype=jnp.float32) * sd, 'bk': jax.random.normal(ks[4], (H,), dtype=jnp.float32) * sd, 'Wv': jax.random.normal(ks[5], (H, H), dtype=jnp.float32) * sd, 'bv': jax.random.normal(ks[6], (H,), dtype=jnp.float32) * sd}
    _L0_attn_in = _L0_attn_setup()

    def _L0_ffn_setup():
        import jax, jax.numpy as jnp
        import numpy as np
        DIM = 128
        DEPTH = 2
        HEADS = 8
        DIM_HEAD = 64
        WINDOW = 64
        INNER = HEADS * DIM_HEAD
        HID = int(DIM * 4 * 2 / 3)
        B, N = (2, 1024)
        QK_SCALE = 8.0

        def shift_token(t):
            t1, t2 = jnp.split(t, 2, axis=-1)
            t2 = jnp.pad(t2, ((0, 0), (1, 0), (0, 0)))[:, :-1]
            return jnp.concatenate([t1, t2], axis=-1)

        def l2norm(t):
            return t / jnp.clip(jnp.linalg.norm(t, axis=-1, keepdims=True), 1e-12)

        def rotate_half(x):
            x1, x2 = jnp.split(x, 2, axis=-1)
            return jnp.concatenate([-x2, x1], axis=-1)

        def rotary_xpos(q, k):
            n = q.shape[-2]
            half_idx = jnp.arange(0, DIM_HEAD, 2, dtype=jnp.float32)
            inv_freq = 1.0 / 10000.0 ** (half_idx / DIM_HEAD)
            t = jnp.arange(n, dtype=jnp.float32)
            freqs = t[:, None] * inv_freq[None, :]
            freqs = jnp.concatenate([freqs, freqs], axis=-1)
            base = (half_idx + 0.4 * DIM_HEAD) / (1.4 * DIM_HEAD)
            power = (t - n // 2) / float(WINDOW // 2)
            scale = base[None, :] ** power[:, None]
            scale = jnp.concatenate([scale, scale], axis=-1)
            cos, sin = (jnp.cos(freqs), jnp.sin(freqs))
            q = q * cos * scale + rotate_half(q) * sin * scale
            k = k * cos / scale + rotate_half(k) * sin / scale
            return (q, k)

        def local_attention(q, k, v):
            b, h, n, d = q.shape
            w = n // WINDOW
            bq = q.reshape(b, h, w, WINDOW, d) * QK_SCALE
            bk = k.reshape(b, h, w, WINDOW, d)
            bv = v.reshape(b, h, w, WINDOW, d)

            def look_around(t):
                p = jnp.pad(t, ((0, 0), (0, 0), (1, 0), (0, 0), (0, 0)))
                return jnp.concatenate([p[:, :, :w], p[:, :, 1:]], axis=3)
            bk, bv = (look_around(bk), look_around(bv))
            bt = jnp.arange(n).reshape(w, WINDOW)
            btp = jnp.pad(bt, ((1, 0), (0, 0)), constant_values=-1)
            btk = jnp.concatenate([btp[:w], btp[1:]], axis=1)
            sim = jnp.einsum('bhwid,bhwjd->bhwij', bq, bk)
            i = bt[:, :, None]
            j = btk[:, None, :]
            mask = (i < j) | (i > j + WINDOW) | (j == -1)
            sim = jnp.where(mask, -jnp.finfo(sim.dtype).max, sim)
            attn = jax.nn.softmax(sim, axis=-1)
            out = jnp.einsum('bhwij,bhwjd->bhwid', attn, bv)
            return out.reshape(b, h, n, d)

        def _layer(x, wqkv, qs, ksc, wo, lg, lb, w1, b1, w2, b2):
            b, n, _ = x.shape
            h = shift_token(x)
            qkv = h @ wqkv
            q, k, v = jnp.split(qkv, 3, axis=-1)
            to_heads = lambda t: t.reshape(b, n, HEADS, DIM_HEAD).transpose(0, 2, 1, 3)
            q, k, v = (to_heads(q), to_heads(k), to_heads(v))
            q = l2norm(q) * qs
            k = l2norm(k) * ksc
            q, k = rotary_xpos(q, k)
            o = local_attention(q, k, v)
            o = o.transpose(0, 2, 1, 3).reshape(b, n, INNER)
            x = x + o @ wo
            h = shift_token(x)
            mu = h.mean(-1, keepdims=True)
            var = h.var(-1, keepdims=True)
            h = (h - mu) / jnp.sqrt(var + 1e-05) * lg + lb
            h = h @ w1 + b1
            a, g = jnp.split(h, 2, axis=-1)
            h = a * jax.nn.gelu(g, approximate=False)
            x = x + h @ w2 + b2
            return x
        key = jax.random.key(seed)
        ks = jax.random.split(key, 6)
        return {'x': jax.random.normal(ks[0], (B, N, DIM), jnp.float32), 'wqkv': jax.random.normal(ks[1], (DEPTH, DIM, 3 * INNER), jnp.float32) * 0.02, 'q_scale': jnp.ones((DEPTH, DIM_HEAD), jnp.float32), 'k_scale': jnp.ones((DEPTH, DIM_HEAD), jnp.float32), 'wo': jax.random.normal(ks[2], (DEPTH, INNER, DIM), jnp.float32) * 0.02, 'ln_g': jnp.ones((DEPTH, DIM), jnp.float32), 'ln_b': jnp.zeros((DEPTH, DIM), jnp.float32), 'w1': jax.random.normal(ks[3], (DEPTH, DIM, 2 * HID), jnp.float32) * 0.02, 'b1': jnp.zeros((DEPTH, 2 * HID), jnp.float32), 'w2': jax.random.normal(ks[4], (DEPTH, HID, DIM), jnp.float32) * 0.02, 'b2': jnp.zeros((DEPTH, DIM), jnp.float32)}
    _L0_ffn_in = _L0_ffn_setup()
    _d = {'L0_attn_hidden_states': _L0_attn_in['hidden_states'], 'L0_attn_Wq': _L0_attn_in['Wq'], 'L0_attn_bq': _L0_attn_in['bq'], 'L0_attn_Wk': _L0_attn_in['Wk'], 'L0_attn_bk': _L0_attn_in['bk'], 'L0_attn_Wv': _L0_attn_in['Wv'], 'L0_attn_bv': _L0_attn_in['bv'], 'L0_ffn_wqkv': _L0_ffn_in['wqkv'], 'L0_ffn_q_scale': _L0_ffn_in['q_scale'], 'L0_ffn_k_scale': _L0_ffn_in['k_scale'], 'L0_ffn_wo': _L0_ffn_in['wo'], 'L0_ffn_ln_g': _L0_ffn_in['ln_g'], 'L0_ffn_ln_b': _L0_ffn_in['ln_b'], 'L0_ffn_w1': _L0_ffn_in['w1'], 'L0_ffn_b1': _L0_ffn_in['b1'], 'L0_ffn_w2': _L0_ffn_in['w2'], 'L0_ffn_b2': _L0_ffn_in['b2']}
    _x0 = _d['L0_attn_hidden_states']
    _d['L0_attn_hidden_states'] = jax.random.normal(jax.random.fold_in(jax.random.key(seed), 1), (2, 1024, 128), dtype=_x0.dtype)
    del _x0
    return _d

def reference(L0_attn_hidden_states, L0_attn_Wq, L0_attn_bq, L0_attn_Wk, L0_attn_bk, L0_attn_Wv, L0_attn_bv, L0_ffn_wqkv, L0_ffn_q_scale, L0_ffn_k_scale, L0_ffn_wo, L0_ffn_ln_g, L0_ffn_ln_b, L0_ffn_w1, L0_ffn_b1, L0_ffn_w2, L0_ffn_b2):

    def _L0_attn_ref(hidden_states, Wq, bq, Wk, bk, Wv, bv):
        import jax, jax.numpy as jnp
        import numpy as np
        import math
        HEAD_SIZE = 64

        def rotate_every_two(x):
            x1 = x[..., ::2]
            x2 = x[..., 1::2]
            return jnp.stack((-x2, x1), axis=-1).reshape(x.shape)

        def rope_table(seq_len, dtype=jnp.float32):
            pos = jnp.arange(seq_len, dtype=jnp.float32)
            inv = 10000.0 ** (jnp.arange(0, HEAD_SIZE, 2, dtype=jnp.float32) / HEAD_SIZE)
            radians = pos[:, None] / inv
            sincos = jnp.stack((jnp.sin(radians), jnp.cos(radians)), axis=-1).reshape(seq_len, -1)
            t = jnp.repeat(sincos, 2, axis=-1)
            return t.astype(dtype)
        B, S, H = hidden_states.shape
        t = rope_table(S, hidden_states.dtype)
        q = hidden_states @ Wq.T + bq
        k = hidden_states @ Wk.T + bk
        v = hidden_states @ Wv.T + bv
        q = q * t + rotate_every_two(q) * t
        k = k * t + rotate_every_two(k) * t
        scale = math.sqrt(HEAD_SIZE)
        scores = jnp.einsum('bsh,bth->bst', q, k) / scale
        probs = jax.nn.softmax(scores, axis=-1)
        out = jnp.einsum('bst,bth->bsh', probs, v)
        return out

    def _L0_ffn_ref(x, wqkv, q_scale, k_scale, wo, ln_g, ln_b, w1, b1, w2, b2):
        import jax, jax.numpy as jnp
        import numpy as np
        DIM = 128
        DEPTH = 2
        HEADS = 8
        DIM_HEAD = 64
        WINDOW = 64
        INNER = HEADS * DIM_HEAD
        HID = int(DIM * 4 * 2 / 3)
        B, N = (2, 1024)
        QK_SCALE = 8.0

        def shift_token(t):
            t1, t2 = jnp.split(t, 2, axis=-1)
            t2 = jnp.pad(t2, ((0, 0), (1, 0), (0, 0)))[:, :-1]
            return jnp.concatenate([t1, t2], axis=-1)

        def l2norm(t):
            return t / jnp.clip(jnp.linalg.norm(t, axis=-1, keepdims=True), 1e-12)

        def rotate_half(x):
            x1, x2 = jnp.split(x, 2, axis=-1)
            return jnp.concatenate([-x2, x1], axis=-1)

        def rotary_xpos(q, k):
            n = q.shape[-2]
            half_idx = jnp.arange(0, DIM_HEAD, 2, dtype=jnp.float32)
            inv_freq = 1.0 / 10000.0 ** (half_idx / DIM_HEAD)
            t = jnp.arange(n, dtype=jnp.float32)
            freqs = t[:, None] * inv_freq[None, :]
            freqs = jnp.concatenate([freqs, freqs], axis=-1)
            base = (half_idx + 0.4 * DIM_HEAD) / (1.4 * DIM_HEAD)
            power = (t - n // 2) / float(WINDOW // 2)
            scale = base[None, :] ** power[:, None]
            scale = jnp.concatenate([scale, scale], axis=-1)
            cos, sin = (jnp.cos(freqs), jnp.sin(freqs))
            q = q * cos * scale + rotate_half(q) * sin * scale
            k = k * cos / scale + rotate_half(k) * sin / scale
            return (q, k)

        def local_attention(q, k, v):
            b, h, n, d = q.shape
            w = n // WINDOW
            bq = q.reshape(b, h, w, WINDOW, d) * QK_SCALE
            bk = k.reshape(b, h, w, WINDOW, d)
            bv = v.reshape(b, h, w, WINDOW, d)

            def look_around(t):
                p = jnp.pad(t, ((0, 0), (0, 0), (1, 0), (0, 0), (0, 0)))
                return jnp.concatenate([p[:, :, :w], p[:, :, 1:]], axis=3)
            bk, bv = (look_around(bk), look_around(bv))
            bt = jnp.arange(n).reshape(w, WINDOW)
            btp = jnp.pad(bt, ((1, 0), (0, 0)), constant_values=-1)
            btk = jnp.concatenate([btp[:w], btp[1:]], axis=1)
            sim = jnp.einsum('bhwid,bhwjd->bhwij', bq, bk)
            i = bt[:, :, None]
            j = btk[:, None, :]
            mask = (i < j) | (i > j + WINDOW) | (j == -1)
            sim = jnp.where(mask, -jnp.finfo(sim.dtype).max, sim)
            attn = jax.nn.softmax(sim, axis=-1)
            out = jnp.einsum('bhwij,bhwjd->bhwid', attn, bv)
            return out.reshape(b, h, n, d)

        def _layer(x, wqkv, qs, ksc, wo, lg, lb, w1, b1, w2, b2):
            b, n, _ = x.shape
            h = shift_token(x)
            qkv = h @ wqkv
            q, k, v = jnp.split(qkv, 3, axis=-1)
            to_heads = lambda t: t.reshape(b, n, HEADS, DIM_HEAD).transpose(0, 2, 1, 3)
            q, k, v = (to_heads(q), to_heads(k), to_heads(v))
            q = l2norm(q) * qs
            k = l2norm(k) * ksc
            q, k = rotary_xpos(q, k)
            o = local_attention(q, k, v)
            o = o.transpose(0, 2, 1, 3).reshape(b, n, INNER)
            x = x + o @ wo
            h = shift_token(x)
            mu = h.mean(-1, keepdims=True)
            var = h.var(-1, keepdims=True)
            h = (h - mu) / jnp.sqrt(var + 1e-05) * lg + lb
            h = h @ w1 + b1
            a, g = jnp.split(h, 2, axis=-1)
            h = a * jax.nn.gelu(g, approximate=False)
            x = x + h @ w2 + b2
            return x
        for l in range(DEPTH):
            x = _layer(x, wqkv[l], q_scale[l], k_scale[l], wo[l], ln_g[l], ln_b[l], w1[l], b1[l], w2[l], b2[l])
        return x
    x = L0_attn_hidden_states
    x = x + _L0_attn_ref(_layernorm(x, axis=-1), L0_attn_Wq, L0_attn_bq, L0_attn_Wk, L0_attn_bk, L0_attn_Wv, L0_attn_bv)
    x = x + _L0_ffn_ref(_layernorm(x, axis=-1), L0_ffn_wqkv, L0_ffn_q_scale, L0_ffn_k_scale, L0_ffn_wo, L0_ffn_ln_g, L0_ffn_ln_b, L0_ffn_w1, L0_ffn_b1, L0_ffn_w2, L0_ffn_b2)
    return x

_drawn_inputs = setup_inputs


def setup_inputs(seed=0):
    import zlib

    import numpy as np

    out = dict(_drawn_inputs(seed))
    spreads = {'L0_ffn_q_scale': (1.0, 0.6),
     'L0_ffn_k_scale': (1.0, 0.6),
     'L0_ffn_ln_g': (1.0, 0.6),
     'L0_ffn_ln_b': (0.0, 0.8),
     'L0_ffn_b1': (0.0, 0.8),
     'L0_ffn_b2': (0.0, 0.447)}
    factors = {'L0_attn_bq': 3.884,
     'L0_attn_bk': 4.317,
     'L0_ffn_wqkv': 3.596,
     'L0_ffn_wo': 3.572,
     'L0_ffn_w1': 6.227,
     'L0_ffn_w2': 6.143}
    for name, (base, spread) in spreads.items():
        noise = np.random.default_rng([zlib.crc32(name.encode()), seed]).standard_normal(out[name].shape)
        drawn = base * np.exp(spread * noise) if base else spread * noise
        out[name] = jnp.asarray(drawn.astype(out[name].dtype))
    for name, factor in factors.items():
        out[name] = (out[name] * factor).astype(out[name].dtype)
    return out
```

```python
from contextlib import ExitStack

import numpy as np

import concourse.bass as bass
from concourse import mybir

F32 = mybir.dt.float32
F32R = mybir.dt.float32r
BF16 = mybir.dt.bfloat16
I32 = mybir.dt.int32
ALU = mybir.AluOpType
ACT = mybir.ActivationFunctionType
AX = mybir.AxisListType

P = 128
B, N, D = 2, 1024, 128
TB = N // P
T = B * TB
DEPTH = 2
H, DH, W = 8, 64, 64
INNER = H * DH
HP = H // 2
HID = int(D * 4 * 2 / 3)
HE = HID + HID % 2
HC = 3
G = T * DEPTH
R = 4
QK_SCALE = 8.0
A_SCALE = 1.0 / 8.0
EPS = 1e-5
NORM_FLOOR2 = 1e-24
RSQRT_SEED = float(0x5F3759DF - 2 ** 30 - 2 ** 22)
MASKED = -1e30
ARENA = 22300

SKEW = dict(h=0, v=1, qkT=2, pT=3, oT=4, hnT=5, w1=6, uT=8)
FILL = 12
LAST = G + SKEW["uT"]


def slot(g):
    return ((g % T) * (TB + 1)) // TB + 1


STEPS_NEWTON = 12
SLOTS = B * (TB + 1)


def constants():
    f = np.float32
    inv = (f(10000.0) ** (np.arange(0, 64, 2, dtype=f) / f(64))).astype(f)
    rad = (np.arange(N, dtype=f)[:, None] / inv).astype(f)
    sincos = np.stack((np.sin(rad), np.cos(rad)), axis=-1).reshape(N, -1)
    rope = np.repeat(sincos, 2, axis=-1).astype(f)
    turn = np.eye(P, dtype=f)
    for i in range(0, P, 2):
        turn[i + 1, i] = -1.0
        turn[i, i + 1] = 1.0
    half = np.arange(0, DH, 2, dtype=f)
    inv_freq = (f(1.0) / f(10000.0) ** (half / f(DH))).astype(f)
    t = np.arange(N, dtype=f)
    freqs = t[:, None] * inv_freq[None, :]
    freqs = np.concatenate([freqs, freqs], axis=-1)
    base = (half + f(0.4 * DH)) / f(1.4 * DH)
    power = (t - N // 2) / f(W // 2)
    scale = (base[None, :] ** power[:, None]).astype(f)
    scale = np.concatenate([scale, scale], axis=-1)
    cos, sin = np.cos(freqs).astype(f), np.sin(freqs).astype(f)
    sign = np.concatenate([-np.ones(DH // 2, f), np.ones(DH // 2, f)])
    tabs = [cos * scale * f(QK_SCALE), sin * scale * sign * f(QK_SCALE), cos / scale, sin / scale * sign]
    xpos = np.stack(tabs).astype(f).reshape(4, TB, P, DH).transpose(2, 0, 1, 3)
    i = (np.arange(P) % W)[:, None]
    r = np.arange(2 * W)[None, :]
    band = (r >= i) & (r <= i + W)
    first = band & ((np.arange(P)[:, None] >= W) | (r >= W))
    mask = np.where(np.stack([first, band], axis=1), 0.0, MASKED).astype(np.float32)
    return {
        "rope": np.ascontiguousarray(rope.T), "turn": turn, "eye": np.eye(P, dtype=f),
        "xpos": np.ascontiguousarray(xpos), "mask": mask,
    }


def build(nc, d, out):
    ctx = ExitStack()
    with ctx:
        def sb(name, shape, dt=F32):
            return ctx.enter_context(nc.sbuf_tensor(name, shape, dt))

        def sem(name):
            return ctx.enter_context(nc.semaphore(name))

        arena = sb("arena", [P, ARENA])
        taken = {"before": 0, "after": 0}

        def place(lot, shape):
            n = int(np.prod(shape[1:]))
            at0 = taken[lot]
            taken[lot] += n + n % 2
            assert taken[lot] <= ARENA, (lot, taken)
            dims = " ".join(f"d{i}" for i in range(len(shape) - 1))
            sizes = {f"d{i}": shape[i + 1] for i in range(1, len(shape) - 1)}
            flat = arena[0:shape[0], at0:at0 + n]
            return flat.rearrange(f"p ({dims}) -> p {dims}", **sizes) if len(shape) > 2 else flat

        def before(name, shape):
            return place("before", shape)

        def after(name, shape):
            return place("after", shape)

        eye = sb("eye", [P, P])
        eye16 = sb("eye16", [P, P], BF16)
        turn = before("turn", [P, P])
        rope = before("rope", [P, N])
        mask32 = before("mask32", [P, 2, 2 * W])
        mask = sb("mask", [P, 2, 4 * 2 * W], BF16)
        xpos = before("xpos", [P, 4, TB, DH])
        scales = before("scales", [P, 2, DEPTH, DH])
        xtab = sb("xtab", [P, 4, DEPTH * TB, DH])
        wa = before("wa", [P, 3, P])
        waT = before("waT", [P, 3, P])
        ba = before("ba", [P, 2])
        baT = before("baT", [P, 2])
        bv = before("bv", [P, P])
        wqkv = before("wqkv", [P, DEPTH, 3 * INNER])
        wqkv_h = sb("wqkv_h", [P, DEPTH, 3 * INNER], F32R)
        wqkv_l = sb("wqkv_l", [P, DEPTH, 3 * INNER], F32R)
        wo = before("wo", [P, DEPTH, 4, P])
        wo_h = sb("wo_h", [P, DEPTH, 4, P], F32R)
        wo_l = sb("wo_l", [P, DEPTH, 4, P], F32R)
        w1 = before("w1", [P, DEPTH, 2, HE])
        w1g = before("w1g", [P, DEPTH, 2, HE])
        w1_h = sb("w1_h", [P, DEPTH, 2, HE], F32R)
        w1_l = sb("w1_l", [P, DEPTH, 2, HE], F32R)
        lng = before("lng", [P, DEPTH])
        lnb = before("lnb", [P, DEPTH, 2])
        b1 = before("b1", [2, DEPTH, 2, HE])
        b1_hl = sb("b1_hl", [2, DEPTH, 2, HE], F32R)
        w2 = sb("w2", [P, DEPTH, HC, P])
        b2 = before("b2", [2, DEPTH, P])
        b2_hl = sb("b2_hl", [2, DEPTH, P], F32R)
        ones2 = sb("ones2", [2, P], F32R)
        ones2f = before("ones2f", [2, P])
        c15 = sb("c15", [P, 2 * H + 1])
        gap = sb("gap", [P, 1])

        x_in = sb("x_in", [P, T, D])
        stats = sb("stats", [P, T, 6])
        mv = sb("mv", [P, T, 2])
        var = sb("var", [P, T])
        rstd = sb("rstd", [P, T])
        newt = sb("newt", [P, T])
        xn = before("xn", [P, 2, D])
        xnT = before("xnT", [P, 2, P])
        qT32 = before("qT32", [P, T, P])
        kT32 = before("kT32", [P, 2, P])
        kTh = sb("kTh", [P, B, N], F32R)
        kTl = sb("kTl", [P, B, N], F32R)
        va = before("va", [P, T, D])
        qh = sb("qh", [P, R, P], F32R)
        ql = sb("ql", [P, R, P], F32R)
        nmax = sb("nmax", [P, 2])
        nbias = sb("nbias", [P, R])
        den = sb("den", [P, R])
        rden = sb("rden", [P, 2])
        pa = before("pa", [P, 2, N])
        paT = before("paT", [P, 2, N])
        b1l = paT[0:2].rearrange("p a n -> p (a n)")[:, 0:2 * DEPTH * HE].rearrange("p (l a n) -> p l a n", l=DEPTH, a=2)
        b2l = pa[0:2].rearrange("p a n -> p (a n)")[:, 0:DEPTH * P].rearrange("p (l n) -> p l n", l=DEPTH)
        x1r = sb("x1r", [P, 2, D])
        x1 = x_in
        mv1 = sb("mv1", [P, R, 2])
        var1 = sb("var1", [P, R])
        rstd1 = sb("rstd1", [P, R])
        newt1 = sb("newt1", [P, R])

        under = kTh[:, :, :].rearrange("p b n -> p (b n)")
        oTh, oTl, hTh, hTl = (under[:, n * 4 * P:(n + 1) * 4 * P] for n in range(4))
        under = kTl[:, :, :].rearrange("p b n -> p (b n)")
        hnTh, hnTl, oTh1, oTl1 = (under[:, n * 4 * P:(n + 1) * 4 * P] for n in range(4))
        oTh, oTh1, oTl, oTl1 = (t.rearrange("p (c n) -> p c n", c=4) for t in (oTh, oTh1, oTl, oTl1))
        oTh, oTl = (oTh, oTh1), (oTl, oTl1)
        hTh, hTl, hnTh, hnTl = (t.rearrange("p (r n) -> p r n", r=R) for t in (hTh, hTl, hnTh, hnTl))
        xs = sb("xs", [P, SLOTS, D])
        x2s = sb("x2s", [P, SLOTS, D])
        h_r = after("h_r", [P, R, D])
        sq = after("sq", [P, 2, INNER])
        t1 = after("t1", [P, 2, INNER])
        t2 = after("t2", [P, 2, INNER])
        qk = after("qk", [P, 2, 2, INNER])
        kn = after("kn", [P, 2, INNER])
        mm = sb("mm", [P, R, 2 * H + 1])
        yy = sb("yy", [P, R, 2 * H + 1])
        n2, rn = mm[:, :, 0:2 * H], yy[:, :, 0:2 * H]
        newt_n = sb("newt_n", [P, 2 * H + 1])
        v_own = after("v_own", [P, R, H, DH + 1])
        v_back = after("v_back", [P, R, H, DH + 1])
        qT = after("qT", [P, 2, HP, P])
        kT = after("kT", [P, HP, W + R * P])
        mx = after("mx", [P, R, H])
        nb = after("nb", [P, R, H])
        pr = after("pr", [P, 2, 2, HP, 2 * W])
        prT = after("prT", [P, 2, HP, P])
        ro = after("ro", [P, 2, 2, HP])
        on = after("on", [P, HP, 2, DH])
        h2_r = after("h2_r", [P, R, D])
        st2 = sb("st2", [P, 2, 6])
        mv2 = sb("mv2", [P, R, 2])
        hn = after("hn", [P, 2, D])
        fa = after("fa", [P, 2, HE])
        fg = after("fg", [P, 2, HE])
        fu = after("fu", [P, R, HC * P])
        fuT = after("fuT", [P, 2, HC, P])

        ps = ctx.enter_context(nc.psum_tensor("ps", [P, 8, 512], F32))

        s_x = [sem(f"s_x{b}") for b in range(B)]
        s_cst = sem("s_cst")
        s_wa = sem("s_wa")
        s_wl = sem("s_wl")
        s_zero = sem("s_zero")
        s_wprep_act = sem("s_wprep_act")
        s_wprep = sem("s_wprep")
        s_wpe = sem("s_wpe")
        s_xtab = sem("s_xtab")
        s_pads = sem("s_pads")
        s_stat = sem("s_stat")
        s_newt0 = sem("s_newt0")
        s_gprep = sem("s_gprep")
        s_var = sem("s_var")
        s_rstd = sem("s_rstd")
        s_xn = sem("s_xn")
        s_axT = sem("s_axT")
        s_axTs = sem("s_axTs")
        s_aqkv = sem("s_aqkv")
        s_aq = sem("s_aq")
        s_ak32 = sem("s_ak32")
        s_ak = sem("s_ak")
        s_akh = sem("s_akh")
        s_aqh = sem("s_aqh")
        s_aql = sem("s_aql")
        s_asc = sem("s_asc")
        s_amx = sem("s_amx")
        s_anb = sem("s_anb")
        s_aex = sem("s_aex")
        s_apT = sem("s_apT")
        s_apTa = sem("s_apTa")
        s_apTd = sem("s_apTd")
        s_apv = sem("s_apv")
        s_ard = sem("s_ard")
        s_ax1 = sem("s_ax1")
        s_ast = sem("s_ast")
        s_amv = sem("s_amv")
        s_aeps = sem("s_aeps")
        s_var1 = sem("s_var1")
        s_newt1 = sem("s_newt1")
        s_rstd1 = sem("s_rstd1")
        p_hT, p_q, p_k, p_v = sem("p_hT"), sem("p_q"), sem("p_k"), sem("p_v")
        p_qT, p_kT, p_sc, p_pT, p_pv = sem("p_qT"), sem("p_kT"), sem("p_sc"), sem("p_pT"), sem("p_pv")
        p_oT, p_wo, p_hnT, p_w1, p_uT, p_w2 = (sem(f"p_{n}") for n in ("oT", "wo", "hnT", "w1", "uT", "w2"))
        a_hTh, a_v, a_sq, a_qT, a_kT, a_exp = (sem(f"a_{n}") for n in ("hTh", "v", "sq", "qT", "kT", "exp"))
        a_pT, a_oTh, a_hnTh, a_g, a_ge, a_uT = (sem(f"a_{n}") for n in ("pT", "oTh", "hnTh", "g", "ge", "uT"))
        d_x, d_hTl, d_t, d_n2, d_nb, d_pT, d_on = (sem(f"d_{n}") for n in ("x", "hTl", "t", "n2", "nb", "pT", "on"))
        d_oTl, d_x2, d_var2, d_hn, d_hnTl, d_a, d_u = (sem(f"d_{n}") for n in ("oTl", "x2", "var2", "hn", "hnTl", "a", "u"))
        d_ns, d_nc, d_mx, d_ro, d_st2, d_mv2, d_eps2 = (sem(f"d_{n}") for n in ("ns", "nc", "mx", "ro", "st2", "mv2", "eps2"))
        s_newtn = sem("s_newtn")
        s_newt2 = sem("s_newt2")
        g_kadd = sem("g_kadd")
        g_q, g_rn, g_k, g_rstd2 = (sem(f"g_{n}") for n in ("q", "rn", "k", "rstd2"))
        m_h = [sem(f"m_h{i}") for i in range(R)]
        m_v = [sem(f"m_v{i}") for i in range(R)]
        m_h2 = [sem(f"m_h2{i}") for i in range(R)]
        s_ready = sem("s_ready")
        s_turn = sem("s_turn")
        s_y = sem("s_y")
        s_out = sem("s_out")

        NLOAD_CST, NLOAD_WA, NLOAD_WL = 6, 6, 16

        block = ctx.enter_context(nc.Block())

        def wait(eng, s, v):
            if not (isinstance(v, int) and v <= 0):
                eng.wait_ge(s, v)

        def split3(eng, o, hi, lo, wh, wl, start=True, stop=True):
            eng.matmul(o, hi, wh, start=start, stop=False)
            eng.matmul(o, hi, wl, start=False, stop=False)
            return eng.matmul(o, lo, wh, start=False, stop=stop)

        def pipeline(eng, step, tiles, fill, last, unroll):
            for j in range(fill):
                step(j, j % unroll)
            with eng.Fori(fill // unroll, tiles // unroll) as i:
                for u in range(unroll):
                    step(i * unroll + u, u)
            for j in range(tiles, last):
                step(j, j % unroll)

        def project(eng, step):
            pipeline(eng, step, T, 4, T + 1, 2)

        def attend(eng, step):
            pipeline(eng, step, T, 8, T + 5, R)

        def stream(eng, step):
            pipeline(eng, step, G, FILL, LAST, R)

        def has(j, skew, tiles=T):
            return not isinstance(j, int) or 0 <= j - skew < tiles

        def newton(gp, y, m, tmp, links, g):
            k = STEPS_NEWTON * g
            for n in range(3):
                gp.tensor_tensor(tmp, y, y, ALU.mult).then_inc(links, 1)
                gp.wait_ge(links, k + 4 * n + 1)
                gp.tensor_tensor(tmp, tmp, m, ALU.mult).then_inc(links, 1)
                gp.wait_ge(links, k + 4 * n + 2)
                gp.tensor_tensor(tmp, tmp, c15[:, 0:tmp.shape[1]], ALU.add).then_inc(links, 1)
                gp.wait_ge(links, k + 4 * n + 3)
                last = gp.tensor_tensor(y, y, tmp, ALU.mult).then_inc(links, 1)
                gp.wait_ge(links, k + 4 * n + 4)

        def at(j, u, stage, off=0):
            k = SKEW[stage] + off
            live = not isinstance(j, int) or 0 <= j - k < G
            return j - k, (u - k) % R, live

        def through(j, stage):
            n = j - SKEW[stage] + 1
            return min(n, G) if isinstance(j, int) else n

        def layer(g):
            return g // T

        def table_row(g):
            return (g // T) * TB + g % TB

        def halves(ap):
            return ap.rearrange("p (h a c) -> p h a c", h=H, a=2)

        @block.sync
        def _(sp):
            sp.dma_start(x_in[:, 0:TB, :], d["x"][0].rearrange("(t p) d -> p t d", p=P)).then_inc(s_x[0], 16)
            sp.dma_start(wa[:, 0, :], d["Wq"]).then_inc(s_wa, 16)
            sp.dma_start(wa[:, 1, :], d["Wk"]).then_inc(s_wa, 16)
            sp.dma_start(wa[:, 2, :], d["Wv"]).then_inc(s_wa, 16)
            sp.dma_start(ba[:, 0:1], d["bq"].rearrange("(p a) -> p a", a=1)).then_inc(s_wa, 16)
            sp.dma_start(ba[:, 1:2], d["bk"].rearrange("(p a) -> p a", a=1)).then_inc(s_wa, 16)
            sp.dma_start(bv[:, :], d["bv"].partition_broadcast(P)).then_inc(s_wa, 16)
            sp.dma_start(eye[:, :], d["eye"]).then_inc(s_cst, 16)
            sp.dma_start(turn[:, :], d["turn"]).then_inc(s_cst, 16)
            sp.dma_start(x_in[:, TB:T, :], d["x"][1].rearrange("(t p) d -> p t d", p=P)).then_inc(s_x[1], 16)
            sp.dma_start(rope[:, :], d["rope"]).then_inc(s_cst, 16)
            sp.dma_start(mask32[:, :, :], d["mask"]).then_inc(s_cst, 16)
            sp.dma_start(xpos[:, :, :, :], d["xpos"]).then_inc(s_cst, 16)
            sp.dma_start(scales[:, :, :, :].rearrange("p a l c -> p (a l c)"),
                         d["scales"].partition_broadcast(P)).then_inc(s_cst, 16)
            sp.wait_ge(s_pads, 3)
            sp.dma_start(wqkv[:, :, :], d["wqkv"].rearrange("l k n -> k l n")).then_inc(s_wl, 16)
            sp.dma_start(wo[:, :, :, :], d["wo"].rearrange("l (c k) n -> k l c n", k=P)).then_inc(s_wl, 16)
            sp.dma_start(lng[:, :], d["ln_g"]).then_inc(s_wl, 16)
            sp.dma_start(lnb[:, :, :], d["ln_b"]).then_inc(s_wl, 16)
            for l in range(DEPTH):
                sp.dma_start(w1[:, l, :, 0:HID], d["w1"][l].rearrange("k (a n) -> k a n", a=2)).then_inc(s_wl, 16)
                sp.dma_start(w2[:, l, 0:2, :], d["w2"][l, 0:2 * P, :].rearrange("(c k) n -> k c n", k=P)).then_inc(s_wl, 16)
                sp.dma_start(w2[0:HID - 2 * P, l, 2, :], d["w2"][l, 2 * P:HID, :]).then_inc(s_wl, 16)
                for r in range(2):
                    sp.dma_start(b1[r:r + 1, l, :, 0:HID], d["b1"][l:l + 1].rearrange("l (a n) -> l a n", a=2)).then_inc(s_wl, 16)
            for r in range(2):
                sp.dma_start(b2[r:r + 1, :, :], d["b2"].rearrange("(a l) n -> a l n", a=1)).then_inc(s_wl, 16)

            def carried(s, v):
                wait(sp, s, v)
                if not isinstance(v, int):
                    sp.sem_inc(s_turn, 1)

            def place_of(g):
                return (slot(g), slot(g) - 1) if isinstance(g, int) else (sp.snap(slot(g)), sp.snap(slot(g) - 1))

            def step(j, u):
                g, s, live = at(j, u, "v")
                if live:
                    carried(a_v, g + 1)
                    carried(p_pv, 2 * (g - R + 1))
                    sp.dma_start(v_back[0:W, s, :, :], v_own[W:P, (s - 1) % R, :, :]).then_inc(m_v[s], 16)
                    sp.dma_start(v_back[W:P, s, :, :], v_own[0:W, s, :, :]).then_inc(m_v[s], 16)
                g, s, live = at(j, u, "h")
                if live:
                    sl, before_sl = place_of(g)
                    carried(d_x, g + 1)
                    carried(p_hT, g - R + 1)
                    sp.dma_start(h_r[:, s, 0:D // 2], xs[:, sl, 0:D // 2]).then_inc(m_h[s], 16)
                    sp.dma_start(h_r[1:P, s, D // 2:D], xs[0:P - 1, sl, D // 2:D]).then_inc(m_h[s], 16)
                    sp.dma_start(h_r[0:1, s, D // 2:D], xs[P - 1:P, before_sl, D // 2:D]).then_inc(m_h[s], 16)
                g, s, live = at(j, u, "oT")
                if live:
                    sl, before_sl = place_of(g)
                    carried(d_x2, g + 1)
                    carried(d_hn, g - R + 1)
                    sp.dma_start(h2_r[:, s, 0:D // 2], x2s[:, sl, 0:D // 2]).then_inc(m_h2[s], 16)
                    sp.dma_start(h2_r[1:P, s, D // 2:D], x2s[0:P - 1, sl, D // 2:D]).then_inc(m_h2[s], 16)
                    sp.dma_start(h2_r[0:1, s, D // 2:D], x2s[P - 1:P, before_sl, D // 2:D]).then_inc(m_h2[s], 16)

            sp.wait_ge(s_zero, 4)
            sp.wait_ge(s_ready, 3)
            stream(sp, step)
            o = out.rearrange("b (t p) d -> p (b t) d", p=P)
            sp.wait_ge(s_y, 1)
            sp.dma_start(o[:, 0:T // 2, :], x1[:, 0:T // 2, :]).then_inc(s_out, 16)
            for t in range(T // 2, T):
                sp.wait_ge(s_y, 2 + t - T // 2)
                sp.dma_start(o[:, t, :], x1[:, t, :]).then_inc(s_out, 16)
            sp.wait_ge(s_out, 16 * (1 + T // 2))

        @block.gpsimd
        def _(gp):
            for t in (w1, w2, b1):
                gp.memset(t[:], 0.0).then_inc(s_pads, 1)
            gp.memset(ones2f[:], 1.0).then_inc(s_zero, 1)
            gp.memset(c15[:], 1.5).then_inc(s_zero, 1)
            for t in (xs, x2s):
                gp.memset(t[:].rearrange("p (b t) d -> p b t d", t=TB + 1)[:, :, 0, :], 0.0).then_inc(s_zero, 1)
            gp.wait_ge(s_zero, 4)
            gp.wait_ge(s_var, 1)
            newton(gp, rstd[:, :], var[:, :], newt[:, :], s_newt0, 0)
            gp.wait_ge(s_wl, 16 * NLOAD_WL)
            for l in range(DEPTH):
                gp.tensor_scalar(w1g[:, l], w1[:, l], lng[:, l:l + 1], 1.0, ALU.mult, ALU.mult).then_inc(s_gprep, 1)
            gp.wait_ge(s_gprep, DEPTH)
            gp.wait_ge(s_wprep_act, 3)
            gp.tensor_tensor(w1_l[:], w1g[:], w1_h[:].bitcast(F32), ALU.subtract)
            gp.wait_ge(s_wprep_act, 4)
            gp.tensor_tensor(wqkv_l[:], wqkv[:], wqkv_h[:].bitcast(F32), ALU.subtract)
            gp.wait_ge(s_wprep_act, 5)
            gp.tensor_tensor(wo_l[:], wo[:], wo_h[:].bitcast(F32), ALU.subtract).then_inc(s_gprep, 1)
            gp.wait_ge(s_cst, 16 * NLOAD_CST)
            for n in range(2):
                gp.tensor_copy(mask[:, n, :].rearrange("p (c r) -> p c r", c=HP),
                               mask32[:, n, :].unsqueeze(1).to_broadcast([P, HP, 2 * W]))
            gp.tensor_copy(eye16[:, :], eye[:, :])
            for a in range(2):
                for l in range(DEPTH):
                    own = scales[:, a, l, :].rearrange("p (b c) -> p b c", b=2)
                    for k, sc in ((2 * a, own), (2 * a + 1, own[:, ::-1, :])):
                        last = gp.tensor_tensor(xtab[:, k, l * TB:(l + 1) * TB, :].rearrange("p t (b c) -> p t b c", b=2),
                                                xpos[:, k, :, :].rearrange("p t (b c) -> p t b c", b=2),
                                                sc.unsqueeze(1).to_broadcast([P, TB, 2, DH // 2]), ALU.mult)
            last.then_inc(s_xtab, 1)

            def astep(j, u):
                if has(j, 4):
                    g, s = j - 4, (u - 4) % R
                    wait(gp, s_var1, g + 1)
                    newton(gp, rstd1[:, s:s + 1], var1[:, s:s + 1], newt1[:, s:s + 1], s_newt1, g)

            attend(gp, astep)
            gp.wait_ge(s_apv, T)
            gp.wait_ge(s_var1, T)
            gp.memset(v_own[:], 1.0).then_inc(s_ready, 1)
            gp.memset(kT[:, :, 0:W], 0.0).then_inc(s_ready, 1)
            gp.memset(fu[:, :, HE:HC * P], 0.0).then_inc(s_ready, 1)

            def step(j, u):
                g, s, live = at(j, u, "h")
                if live:
                    r = s % 2
                    wait(gp, d_t, 2 * g + 1)
                    gp.tensor_tensor(qk[:, r, 1, :], t1[:, 1, :], t2[:, 1, :], ALU.add).then_inc(g_kadd, 1)
                    wait(gp, d_t, 2 * g + 2)
                    wait(gp, p_qT, g - 1)
                    gp.tensor_tensor(qk[:, r, 0, :], t1[:, 0, :], t2[:, 0, :], ALU.add).then_inc(g_q, 1)
                _, _, normed = at(j, u, "oT")
                if live or normed:
                    c = slice(0 if live else 2 * H, 2 * H + 1 if normed else 2 * H)
                    if live:
                        wait(gp, d_n2, g + 1)
                    if normed:
                        wait(gp, d_var2, through(j, "oT"))
                    newton(gp, yy[:, u, c], mm[:, u, c], newt_n[:, c], s_newtn, j)
                if live:
                    wait(gp, g_kadd, g + 1)
                    wait(gp, p_kT, g - 1)
                    gp.tensor_tensor(kn[:, r, :].rearrange("p (h c) -> p h c", h=H),
                                     qk[:, r, 1, :].rearrange("p (h c) -> p h c", h=H),
                                     rn[:, s, H:2 * H].unsqueeze(2).to_broadcast([P, H, DH]), ALU.mult).then_inc(g_k, 1)

            stream(gp, step)

        @block.scalar
        def _(act):
            act.wait_ge(s_wpe, 1)
            act.activation(waT[:, :, :], ps[:, 0, 0:3 * P].rearrange("p (a n) -> p a n", a=3), ACT.Copy).then_inc(s_wprep_act, 1)
            act.activation(baT[:, :], ps[:, 0, 3 * P:3 * P + 2], ACT.Copy).then_inc(s_wprep_act, 1)

            def pstep(j, u):
                if has(j, 0):
                    wait(act, s_axT, j + 1)
                    wait(act, s_aqkv, j - 1)
                    act.activation(xnT[:, u, :], ps[:, 2 + u, 0:P], ACT.Copy).then_inc(s_axTs, 1)

            project(act, pstep)

            act.wait_ge(s_gprep, DEPTH)
            act.activation(w1_h[:], w1g[:], ACT.Copy).then_inc(s_wprep_act, 1)
            act.activation(wqkv_h[:], wqkv[:], ACT.Copy).then_inc(s_wprep_act, 1)
            act.activation(wo_h[:], wo[:], ACT.Copy).then_inc(s_wprep_act, 1)
            act.wait_ge(s_zero, 1)
            act.activation(ones2[:], ones2f[:], ACT.Copy).then_inc(s_wprep_act, 1)

            def astep(j, u):
                if has(j, 2):
                    g, s = j - 2, (u - 2) % 2
                    wait(act, s_apT, g + 1)
                    wait(act, s_apv, g - 1)
                    act.activation(paT[:, s, 0:512], ps[:, 4, :], ACT.Copy).then_inc(s_apTa, 1)
                if has(j, 1):
                    g, s = j - 1, (u - 1) % R
                    b = 2 * (s % 2)
                    wait(act, s_anb, g + 1)
                    wait(act, s_apT, g - 1)
                    act.activation(pa[:, s % 2, :].rearrange("p (a n) -> p a n", a=2), ps[:, b:b + 2, :], ACT.Exp,
                                   bias=nbias[:, s:s + 1], scale=A_SCALE, accum_out=den[:, s:s + 1]).then_inc(s_aex, 1)

            attend(act, astep)
            act.wait_ge(s_ready, 3)

            def step(j, u):
                g, s, live = at(j, u, "qkT")
                if live:
                    wait(act, p_qT, g + 1)
                    act.activation(qT[:, s % 2, :, :], ps[:, 4, :].rearrange("p (c n) -> p c n", c=HP), ACT.Copy).then_inc(a_qT, 1)
                    wait(act, p_kT, g + 1)
                    k_ps = ps[:, 5, :].rearrange("p (c n) -> p c n", c=HP)
                    last = act.activation(kT[:, :, W + s * P:W + (s + 1) * P], k_ps, ACT.Copy)
                    if s == R - 1:
                        last = act.activation(kT[:, :, 0:W], k_ps[:, :, W:P], ACT.Copy)
                    last.then_inc(a_kT, 1)
                g, s, live = at(j, u, "oT")
                if live:
                    wait(act, p_oT, g + 1)
                    wait(act, p_wo, g - 1)
                    act.activation(oTh[s % 2], ps[:, 3, :].rearrange("p (c n) -> p c n", c=4), ACT.Copy).then_inc(a_oTh, 1)
                g, s, live = at(j, u, "w1")
                if live:
                    wait(act, p_w1, g + 1)
                    wait(act, d_u, g // 2)
                    act.activation(fg[:, s % 2, :], ps[:, 2, 0:HE], ACT.Copy).then_inc(a_g, 1)
                g, s, live = at(j, u, "h")
                if live:
                    wait(act, p_hT, g + 1)
                    act.activation(hTh[:, s, :], ps[:, 0, 0:P], ACT.Copy).then_inc(a_hTh, 1)
                g, s, live = at(j, u, "qkT")
                if live:
                    for b in range(2):
                        wait(act, d_nb, 2 * g + b + 1)
                        for c in range(HP):
                            h = 2 * c + b
                            last = act.activation(pr[:, s % 2, b, c, :], ps[:, 6 + b, c * P:(c + 1) * P], ACT.Exp,
                                                  bias=nb[:, s, b * HP + c:b * HP + c + 1], scale=rn[:, s, h:h + 1])
                        last.then_inc(a_exp, 1)
                g, s, live = at(j, u, "uT")
                if live:
                    wait(act, p_uT, g + 1)
                    act.activation(fuT[:, s % 2, :, :], ps[:, 1, 0:HC * P].rearrange("p (c n) -> p c n", c=HC), ACT.Copy).then_inc(a_uT, 1)
                g, s, live = at(j, u, "h")
                if live:
                    wait(act, p_v, g + 1)
                    wait(act, p_pv, 2 * (g - R + 1))
                    if not isinstance(g, int) or g >= R:
                        wait(act, m_v[(s + 1) % R], 2 * 16 * ((g - R + 1) // R + 1))
                    act.activation(v_own[:, s, :, 0:DH], ps[:, 3, :].rearrange("p (h c) -> p h c", h=H), ACT.Copy).then_inc(a_v, 1)
                g, s, live = at(j, u, "hnT")
                if live:
                    wait(act, p_hnT, g + 1)
                    act.activation(hnTh[:, s, :], ps[:, 0, 2 * P:3 * P], ACT.Copy).then_inc(a_hnTh, 1)
                g, s, live = at(j, u, "pT")
                if live:
                    wait(act, p_pT, 2 * g + 1)
                    act.activation(prT[:, 0, :, :], ps[:, 4, :].rearrange("p (c n) -> p c n", c=HP), ACT.Copy).then_inc(a_pT, 1)
                g, s, live = at(j, u, "h")
                if live:
                    wait(act, d_n2, g)
                    wait(act, d_t, 2 * g + 1)
                    act.activation(sq[:, 1, :], ps[:, 2, :], ACT.Square).then_inc(a_sq, 1)
                    wait(act, d_t, 2 * g + 2)
                    act.activation(sq[:, 0, :], ps[:, 1, :], ACT.Square).then_inc(a_sq, 1)
                g, s, live = at(j, u, "w1")
                if live and s % 2 == 1:
                    wait(act, a_g, g + 1)
                    act.activation(fg[:, :, :], fg[:, :, :], ACT.Gelu).then_inc(a_ge, 1)

            stream(act, step)

        @block.vector
        def _(dve):
            def seed(y, x):
                return dve.tensor_scalar(y.bitcast(I32), x.bitcast(I32), -0.5, RSQRT_SEED, ALU.mult, ALU.add)

            for t in range(T):
                if t % TB == 0:
                    dve.wait_ge(s_x[t // TB], 16)
                dve.bn_stats(stats[:, t, :], x_in[:, t, :]).then_inc(s_stat, 1)
            for t in range(T):
                dve.wait_ge(s_stat, t + 1)
                dve.bn_aggr(mv[:, t, :], stats[:, t, :]).then_inc(s_stat, 1)
            dve.wait_ge(s_stat, 2 * T)
            dve.tensor_scalar(var[:, :], mv[:, :, 1], EPS, -0.5, ALU.add, ALU.mult).then_inc(s_stat, 1)
            dve.wait_ge(s_stat, 2 * T + 1)
            seed(rstd[:, :], var[:, :]).then_inc(s_var, 1)
            dve.wait_ge(s_newt0, STEPS_NEWTON)
            dve.wait_ge(s_cst, 16 * NLOAD_CST)
            dve.wait_ge(s_wa, 16 * NLOAD_WA)
            dve.wait_ge(s_wprep_act, 2)

            def pstep(j, u):
                if has(j, 0):
                    wait(dve, s_axT, j - 1)
                    dve.tensor_scalar(xn[:, u, :], x_in[:, bass.ds(j, 1), :].rearrange("p a d -> p (a d)"),
                                      mv[:, bass.ds(j, 1), 0], rstd[:, bass.ds(j, 1)],
                                      ALU.subtract, ALU.mult).then_inc(s_xn, 1)
                if has(j, 1):
                    g, s = j - 1, (u - 1) % 2
                    p = g % TB
                    qkv = ps[:, 4 + s, :]
                    wait(dve, s_aqkv, g + 1)
                    dve.scalar_tensor_tensor(kT32[:, s, :], qkv[:, P:2 * P], baT[:, 1:2],
                                             rope[:, bass.ds(p * P, P)], ALU.add, ALU.mult).then_inc(s_ak32, 1)
                    dve.scalar_tensor_tensor(qT32[:, bass.ds(g, 1), :].rearrange("p a n -> p (a n)"), qkv[:, 0:P], baT[:, 0:1],
                                             rope[:, bass.ds(p * P, P)], ALU.add, ALU.mult).then_inc(s_aq, 1)
                    wait(dve, s_ak32, g + 1)
                    kh = kTh[:, :, :].rearrange("p b n -> p (b n)")[:, bass.ds(g * P, P)]
                    kl = kTl[:, :, :].rearrange("p b n -> p (b n)")[:, bass.ds(g * P, P)]
                    dve.tensor_scalar(kh, kT32[:, s, :], 1.0, None, ALU.mult).then_inc(s_akh, 1)
                    dve.tensor_tensor(va[:, bass.ds(g, 1), :].rearrange("p a n -> p (a n)"), qkv[:, 2 * P:3 * P], bv[:, :], ALU.add)
                    wait(dve, s_akh, g + 1)
                    dve.tensor_tensor(kl, kT32[:, s, :], kh.bitcast(F32), ALU.subtract).then_inc(s_ak, 1)

            project(dve, pstep)

            dve.wait_ge(s_wpe, 2)
            dve.tensor_tensor(b1[:].rearrange("p l a n -> p (l a) n"), b1[:].rearrange("p l a n -> p (l a) n"),
                              ps[0:2, 0:4, 0:HE], ALU.add).then_inc(s_wprep, 1)
            dve.wait_ge(s_wprep, 1)
            dve.tensor_copy(b1_hl[:], b1[:]).then_inc(s_wprep, 1)
            dve.tensor_copy(b2_hl[:], b2[:]).then_inc(s_wprep, 1)
            dve.wait_ge(s_wprep, 3)
            dve.tensor_tensor(b1l[:], b1[:], b1_hl[:].bitcast(F32), ALU.subtract).then_inc(s_wprep, 1)
            dve.tensor_tensor(b2l[:], b2[:], b2_hl[:].bitcast(F32), ALU.subtract).then_inc(s_wprep, 1)
            dve.wait_ge(s_wprep, 5)
            dve.tensor_scalar(b1l[:], b1l[:], eye[0:2, 1:2], None, ALU.mult).then_inc(s_wprep, 1)
            dve.tensor_scalar(b2l[:], b2l[:], eye[0:2, 1:2], None, ALU.mult).then_inc(s_wprep, 1)
            dve.wait_ge(s_wprep, 7)
            flat = "p l a n -> p (l a n)"
            dve.scalar_tensor_tensor(b1_hl[:].rearrange(flat), b1_hl[:].bitcast(F32).rearrange(flat), eye[0:2, 0:1],
                                     b1l[:].rearrange(flat), ALU.mult, ALU.add)
            flat = "p l n -> p (l n)"
            dve.scalar_tensor_tensor(b2_hl[:].rearrange(flat), b2_hl[:].bitcast(F32).rearrange(flat), eye[0:2, 0:1],
                                     b2l[:].rearrange(flat), ALU.mult, ALU.add).then_inc(s_wprep, 1)
            dve.wait_ge(s_zero, 4)

            def astep(j, u):
                if has(j, 0):
                    q = qT32[:, bass.ds(j, 1), :].rearrange("p a n -> p (a n)")
                    wait(dve, s_asc, j - R + 1)
                    dve.tensor_scalar(qh[:, u, :], q, 1.0, None, ALU.mult).then_inc(s_aqh, 1)
                    wait(dve, s_aqh, j + 1)
                    dve.tensor_tensor(ql[:, u, :], q, qh[:, u, :].bitcast(F32), ALU.subtract).then_inc(s_aql, 1)
                if has(j, 4):
                    g, s = j - 4, (u - 4) % R
                    x1g = x1r[:, s % 2, :]
                    wait(dve, s_apv, g + 1)
                    dve.reciprocal(rden[:, s % 2:s % 2 + 1], den[:, s:s + 1]).then_inc(s_ard, 1)
                    wait(dve, s_ard, g + 1)
                    dve.scalar_tensor_tensor(x1g, ps[:, 6 + s % 2, 0:P], rden[:, s % 2:s % 2 + 1],
                                             x_in[:, bass.ds(g, 1), :].rearrange("p a n -> p (a n)"),
                                             ALU.mult, ALU.add).then_inc(s_ax1, 1)
                    wait(dve, s_ax1, g + 1)
                    dve.bn_stats(stats[:, s, :], x1g).then_inc(s_ast, 1)
                    wait(dve, s_ast, g + 1)
                    dve.memset(gap[:, :], 0.0)
                    dve.bn_aggr(mv1[:, s, :], stats[:, s, :]).then_inc(s_amv, 1)
                    wait(dve, s_amv, g + 1)
                    dve.tensor_scalar(var1[:, s:s + 1], mv1[:, s, 1:2], EPS, -0.5, ALU.add, ALU.mult).then_inc(s_aeps, 1)
                    wait(dve, s_aeps, g + 1)
                    seed(rstd1[:, s:s + 1], var1[:, s:s + 1]).then_inc(s_var1, 1)
                    dve.tensor_scalar(x1[:, bass.ds(g, 1), :].rearrange("p a n -> p (a n)"), x1g, 1.0, None, ALU.mult)
                if has(j, 1):
                    g, s = j - 1, (u - 1) % R
                    b = 2 * (s % 2)
                    wait(dve, s_asc, g + 1)
                    dve.tensor_reduce(out=nmax[:, s % 2:s % 2 + 1], in_=ps[:, b:b + 2, :], axis=AX.XY, op=ALU.max,
                                      negate=True).then_inc(s_amx, 1)
                    wait(dve, s_amx, g + 1)
                    dve.tensor_scalar(nbias[:, s:s + 1], nmax[:, s % 2:s % 2 + 1], A_SCALE, None, ALU.mult).then_inc(s_anb, 1)
                if has(j, 2):
                    g, s = j - 2, (u - 2) % 2
                    wait(dve, s_apT, g + 1)
                    wait(dve, s_apv, g - 1)
                    dve.tensor_copy(paT[:, s, 512:1024], ps[:, 5, :]).then_inc(s_apTd, 1)
                if has(j, 5):
                    g, s = j - 5, (u - 5) % R
                    wait(dve, s_newt1, STEPS_NEWTON * (g + 1))
                    dve.tensor_scalar(xs[:, bass.ds(slot(g), 1), :].rearrange("p a n -> p (a n)"),
                                      x1r[:, s % 2, :],
                                      mv1[:, s, 0:1], rstd1[:, s:s + 1], ALU.subtract, ALU.mult).then_inc(d_x, 1)

            attend(dve, astep)
            dve.wait_ge(s_xtab, 1)
            dve.wait_ge(s_ready, 3)

            def tile_of(t, i):
                return t[:, bass.ds(i, 1), :].rearrange("p a n -> p (a n)")

            def products(g, a, ready, bank):
                row = table_row(g)
                wait(dve, ready, g + 1)
                wait(dve, (g_q, g_kadd)[a], g)
                dve.tensor_tensor(t1[:, a, :].rearrange("p (h c) -> p h c", h=H),
                                  ps[:, bank, :].rearrange("p (h c) -> p h c", h=H),
                                  xtab[:, 2 * a, bass.ds(row, 1), :].to_broadcast([P, H, DH]), ALU.mult)
                dve.tensor_tensor(halves(t2[:, a, :]), halves(ps[:, bank, :])[:, :, ::-1, :],
                                  xtab[:, 2 * a + 1, bass.ds(row, 1), :].rearrange("p o (b c) -> p o b c", b=2)
                                  .to_broadcast([P, H, 2, DH // 2]), ALU.mult).then_inc(d_t, 1)

            def step(j, u):
                g, s, live = at(j, u, "oT")
                if live:
                    r = s % 2
                    wait(dve, a_oTh, g + 1)
                    wait(dve, p_wo, g - 1)
                    dve.tensor_tensor(oTl[s % 2], ps[:, 3, :].rearrange("p (c n) -> p c n", c=4),
                                      oTh[s % 2].bitcast(F32), ALU.subtract).then_inc(d_oTl, 1)
                g, s, live = at(j, u, "w1")
                if live:
                    wait(dve, p_w1, g + 1)
                    wait(dve, d_u, g // 2)
                    dve.tensor_copy(fa[:, s % 2, :], ps[:, 1, 0:HE]).then_inc(d_a, 1)
                g, s, live = at(j, u, "h")
                if live:
                    wait(dve, a_hTh, g + 1)
                    dve.tensor_tensor(hTl[:, s, :], ps[:, 0, 0:P], hTh[:, s, :].bitcast(F32), ALU.subtract).then_inc(d_hTl, 1)
                g, s, live = at(j, u, "hnT")
                if live:
                    wait(dve, s_newtn, STEPS_NEWTON * (g + SKEW["oT"] + 1))
                    dve.tensor_scalar(hn[:, s % 2, :], h2_r[:, s, :], mv2[:, s, 0:1], yy[:, (u - 1) % R, 2 * H:2 * H + 1],
                                      ALU.subtract, ALU.mult).then_inc(d_hn, 1)
                g, s, live = at(j, u, "qkT")
                if live:
                    for b in range(2):
                        wait(dve, p_sc, 2 * g + b + 1)
                        dve.tensor_reduce(out=mx[:, s, b * HP:(b + 1) * HP], in_=ps[:, 6 + b, :].rearrange("p (c n) -> p c n", c=HP),
                                          axis=AX.X, op=ALU.max).then_inc(d_mx, 1)
                        wait(dve, d_mx, 2 * g + b + 1)
                        dve.scalar_tensor_tensor(nb[:, s, b * HP:(b + 1) * HP], mx[:, s, b * HP:(b + 1) * HP], -1.0,
                                                 rn[:, s, b:H:2], ALU.mult, ALU.mult).then_inc(d_nb, 1)
                g, s, live = at(j, u, "oT")
                if live:
                    wait(dve, p_wo, g + 1)
                    dve.tensor_tensor(tile_of(x2s, slot(g)), ps[:, 0, P:2 * P], tile_of(xs, slot(g)), ALU.add).then_inc(d_x2, 1)
                g, s, live = at(j, u, "h")
                if live:
                    products(g, 1, p_k, 2)
                g, s, live = at(j, u, "hnT")
                if live:
                    wait(dve, a_hnTh, g + 1)
                    dve.tensor_tensor(hnTl[:, s, :], ps[:, 0, 2 * P:3 * P], hnTh[:, s, :].bitcast(F32), ALU.subtract).then_inc(d_hnTl, 1)
                g, s, live = at(j, u, "h")
                if live:
                    products(g, 0, p_q, 1)
                g, s, live = at(j, u, "pT")
                if live:
                    wait(dve, p_pT, 2 * g + 2)
                    dve.tensor_copy(prT[:, 1, :, :], ps[:, 5, :].rearrange("p (c n) -> p c n", c=HP)).then_inc(d_pT, 1)
                g, s, live = at(j, u, "uT")
                if live:
                    wait(dve, p_w2, g + 1)
                    dve.tensor_tensor(tile_of(xs, slot(g + T)), ps[:, 0, 3 * P:4 * P], tile_of(x2s, slot(g)), ALU.add).then_inc(d_x, 1)
                g, s, live = at(j, u, "pT")
                if live:
                    for b in range(2):
                        wait(dve, p_pv, 2 * g + b + 1)
                        o = ps[:, 4 + b, 0:HP * (DH + 1)].rearrange("p (c n) -> p c n", c=HP)
                        dve.reciprocal(ro[:, s % 2, b, :], o[:, :, DH]).then_inc(d_ro, 1)
                        wait(dve, d_ro, 2 * g + b + 1)
                        dve.tensor_tensor(on[:, :, b, :], o[:, :, 0:DH],
                                          ro[:, s % 2, b, :].unsqueeze(2).to_broadcast([P, HP, DH]), ALU.mult).then_inc(d_on, 1)
                g, s, live = at(j, u, "h")
                if live:
                    wait(dve, a_sq, 2 * g + 2)
                    dve.tensor_reduce(out=n2[:, s, :], in_=sq[:].rearrange("p a (h c) -> p (a h) c", h=H), axis=AX.X,
                                      op=ALU.add).then_inc(d_ns, 1)
                    wait(dve, d_ns, g + 1)
                    dve.tensor_scalar(n2[:, s, :], n2[:, s, :], NORM_FLOOR2, -0.5, ALU.max, ALU.mult).then_inc(d_nc, 1)
                    wait(dve, d_nc, g + 1)
                    seed(rn[:, s, :], n2[:, s, :]).then_inc(d_n2, 1)
                g, s, live = at(j, u, "oT")
                if live:
                    wait(dve, m_h2[s], 3 * 16 * (g // R + 1))
                    dve.bn_stats(st2[:, s % 2, :], h2_r[:, s, :]).then_inc(d_st2, 1)
                    wait(dve, d_st2, g + 1)
                    dve.memset(gap[:, :], 0.0)
                    dve.bn_aggr(mv2[:, s, :], st2[:, s % 2, :]).then_inc(d_mv2, 1)
                    wait(dve, d_mv2, g + 1)
                    dve.tensor_scalar(mm[:, u, 2 * H:2 * H + 1], mv2[:, s, 1:2], EPS, -0.5, ALU.add, ALU.mult).then_inc(d_eps2, 1)
                    wait(dve, d_eps2, g + 1)
                    seed(yy[:, u, 2 * H:2 * H + 1], mm[:, u, 2 * H:2 * H + 1]).then_inc(d_var2, 1)
                g, s, live = at(j, u, "w1")
                if live and s % 2 == 1:
                    wait(dve, a_ge, (g + 1) // 2)
                    dve.tensor_tensor(fu[:, s - 1:s + 1, 0:HE], fa[:, :, :], fg[:, :, :], ALU.mult).then_inc(d_u, 1)
                if isinstance(j, int) and j >= G:
                    last = j - SKEW["uT"] - T
                    outs = [(last, last + 1)]
                    if j == G:
                        outs = [(0, T // 2)] + [(t, t + 1) for t in range(T // 2, last + 1)]
                    for a, b in outs:
                        if a < b:
                            wait(dve, d_x, 2 * T + b)
                            base = slot(a)
                            dve.tensor_tensor(x1[:, a:b, :], x1[:, a:b, :], xs[:, base:base + b - a, :], ALU.add).then_inc(s_y, 1)

            stream(dve, step)

        @block.tensor
        def _(pe):
            pe.wait_ge(s_cst, 16 * NLOAD_CST)
            pe.wait_ge(s_wa, 16 * NLOAD_WA)
            for a in range(2):
                pe.matmul(ps[:, 0, a * P:(a + 1) * P], wa[:, a, :], turn[:, :], start=True, stop=True)
                pe.matmul(ps[:, 0, 3 * P + a:3 * P + a + 1], turn[:, :], ba[:, a:a + 1], start=True, stop=True)
            pe.transpose(ps[:, 0, 2 * P:3 * P], wa[:, 2, :], eye[:, :]).then_inc(s_wpe, 1)
            pe.wait_ge(s_wprep_act, 1)

            def pstep(j, u):
                if has(j, 0):
                    wait(pe, s_xn, j + 1)
                    wait(pe, s_axTs, j - 1)
                    pe.transpose(ps[:, 2 + u, 0:P], xn[:, u, :], eye[:, :]).then_inc(s_axT, 1)
                if has(j, 1):
                    g, s = j - 1, (u - 1) % 2
                    wait(pe, s_axTs, g + 1)
                    wait(pe, s_ak, g - 1)
                    pe.matmul(ps[:, 4 + s, 0:P], waT[:, 0, :], xnT[:, s, :], start=True, stop=True)
                    pe.matmul(ps[:, 4 + s, P:2 * P], waT[:, 1, :], xnT[:, s, :], start=True, stop=True)
                    pe.matmul(ps[:, 4 + s, 2 * P:3 * P], xnT[:, s, :], waT[:, 2, :], start=True, stop=True).then_inc(s_aqkv, 1)

            project(pe, pstep)

            pe.wait_ge(s_wl, 16 * NLOAD_WL)
            pe.wait_ge(s_axTs, T)
            for l in range(DEPTH):
                for a in range(2):
                    last = pe.matmul(ps[0:2, 2 * l + a, 0:HE], lnb[:, l, :], w1[:, l, a, :], start=True, stop=True)
            last.then_inc(s_wpe, 1)
            pe.wait_ge(s_ak, T)
            pe.wait_ge(s_wprep, 8)

            def astep(j, u):
                if has(j, 1):
                    g, s = j - 1, (u - 1) % R
                    wait(pe, s_aql, g + 1)
                    wait(pe, s_aex, g - 1)
                    for n in range(2):
                        cols = bass.ds((g // TB) * N + n * 512, 512)
                        last = split3(pe, ps[:, 2 * (s % 2) + n, :], qh[:, s, :], ql[:, s, :],
                                      kTh[:, :, :].rearrange("p b n -> p (b n)")[:, cols],
                                      kTl[:, :, :].rearrange("p b n -> p (b n)")[:, cols])
                    last.then_inc(s_asc, 1)
                if has(j, 2):
                    g, s = j - 2, (u - 2) % 2
                    wait(pe, s_aex, g + 1)
                    wait(pe, s_apTa, g)
                    wait(pe, s_apTd, g)
                    for c in range(TB):
                        last = pe.transpose(ps[:, 4 + c // 4, (c % 4) * P:(c % 4 + 1) * P], pa[:, s, c * P:(c + 1) * P], eye[:, :])
                    last.then_inc(s_apT, 1)
                if has(j, 3):
                    g, s = j - 3, (u - 3) % 2
                    wait(pe, s_apTa, g + 1)
                    wait(pe, s_apTd, g + 1)
                    wait(pe, s_var1, g - 1)
                    for c in range(TB):
                        last = pe.matmul(ps[:, 6 + s, 0:P], paT[:, s, c * P:(c + 1) * P],
                                         va[:, bass.ds((g // TB) * TB + c, 1), :].rearrange("p a n -> p (a n)"),
                                         start=(c == 0), stop=(c == TB - 1))
                    last.then_inc(s_apv, 1)

            attend(pe, astep)
            pe.wait_ge(s_gprep, DEPTH + 1)
            pe.wait_ge(s_xtab, 1)
            pe.wait_ge(s_wprep_act, 6)
            pe.wait_ge(s_ready, 3)
            pe.wait_ge(s_apTa, T)
            pe.wait_ge(s_apTd, T)
            pe.wait_ge(s_var1, T)

            def row_of(t, *idx):
                l = idx[0]
                return t[(slice(None), bass.ds(l, 1)) + idx[1:]]

            def step(j, u):
                g, s, live = at(j, u, "qkT")
                if live:
                    r = s % 2
                    wait(pe, g_q, g + 1)
                    wait(pe, d_on, 2 * through(j - 1, "pT") - 1)
                    for c in range(HP):
                        last = pe.transpose(ps[:, 4, c * P:(c + 1) * P], qk[:, r, 0, c * P:(c + 1) * P], eye[:, :])
                    last.then_inc(p_qT, 1)
                    wait(pe, g_k, g + 1)
                    wait(pe, d_on, 2 * through(j - 1, "pT"))
                    for c in range(HP):
                        last = pe.transpose(ps[:, 5, c * P:(c + 1) * P], kn[:, r, c * P:(c + 1) * P], eye[:, :])
                    last.then_inc(p_kT, 1)
                g, s, live = at(j, u, "oT")
                if live:
                    wait(pe, d_on, 2 * g + 2)
                    wait(pe, a_v, through(j - 1, "h"))
                    for c in range(4):
                        last = pe.transpose(ps[:, 3, c * P:(c + 1) * P],
                                            on[:, c, :, :].rearrange("p b n -> p (b n)"), eye[:, :])
                    last.then_inc(p_oT, 1)
                g, s, live = at(j, u, "w1")
                if live:
                    wait(pe, d_hnTl, g + 1)
                    wait(pe, d_t, 2 * through(j - 1, "h"))
                    wait(pe, a_sq, 2 * through(j - 1, "h"))
                    l = layer(g)
                    for a in range(2):
                        o = ps[:, 1 + a, 0:HE]
                        pe.matmul(o, ones2[:, :], b1_hl[:, bass.ds(l, 1), a, :].rearrange("p o n -> p (o n)"), start=True, stop=False)
                        last = split3(pe, o, hnTh[:, s, :], hnTl[:, s, :],
                                      w1_h[:, bass.ds(l, 1), a, :].rearrange("p o n -> p (o n)"),
                                      w1_l[:, bass.ds(l, 1), a, :].rearrange("p o n -> p (o n)"), start=False)
                    last.then_inc(p_w1, 1)
                g, s, live = at(j, u, "h")
                if live:
                    wait(pe, m_h[s], 3 * 16 * (g // R + 1))
                    wait(pe, d_x, T + through(j - 1, "uT"))
                    pe.transpose(ps[:, 0, 0:P], h_r[:, s, :], eye[:, :]).then_inc(p_hT, 1)
                g, s, live = at(j, u, "qkT")
                if live:
                    for b in range(2):
                        wait(pe, a_qT, g + 1)
                        wait(pe, a_kT, g + 1)
                        wait(pe, a_exp, 2 * g - 1 + b)
                        first = (g % TB + TB - 1) // TB
                        pe.matmul(ps[:, 6 + b, :], eye16[:, :], mask[:, bass.ds(first, 1), :].rearrange("p o n -> p (o n)"),
                                  start=True, stop=False, skip_group_check=True)
                        rows = slice(DH * b, DH * (b + 1))
                        for c in range(HP):
                            for w in range(2):
                                last = pe.matmul(ps[W * w:W * (w + 1), 6 + b, c * P:(c + 1) * P],
                                                 qT[rows, s % 2, c, W * w:W * (w + 1)],
                                                 kT[rows, c, s * P + W * w:s * P + W * w + 2 * W],
                                                 start=False, stop=True, skip_group_check=True)
                        last.then_inc(p_sc, 1)
                g, s, live = at(j, u, "oT")
                if live:
                    wait(pe, d_oTl, g + 1)
                    wait(pe, d_hTl, through(j, "h"))
                    l = layer(g)
                    for c in range(4):
                        last = split3(pe, ps[:, 0, P:2 * P], oTh[s % 2][:, c, :], oTl[s % 2][:, c, :],
                                      wo_h[:, bass.ds(l, 1), c, :].rearrange("p o n -> p (o n)"),
                                      wo_l[:, bass.ds(l, 1), c, :].rearrange("p o n -> p (o n)"), start=c == 0, stop=c == 3)
                    last.then_inc(p_wo, 1)
                g, s, live = at(j, u, "uT")
                if live:
                    wait(pe, d_u, g // 2 + 1)
                    wait(pe, d_a, through(j, "w1"))
                    for c in range(HC):
                        last = pe.transpose(ps[:, 1, c * P:(c + 1) * P], fu[:, s, c * P:(c + 1) * P], eye[:, :])
                    last.then_inc(p_uT, 1)
                g, s, live = at(j, u, "h")
                if live:
                    wait(pe, d_hTl, g + 1)
                    l = layer(g)
                    for bank, n, done in ((3, 2, p_v), (2, 1, p_k), (1, 0, p_q)):
                        if bank == 3:
                            wait(pe, d_oTl, through(j, "oT"))
                        if bank == 2:
                            wait(pe, a_g, through(j, "w1"))
                        if bank == 1:
                            wait(pe, a_uT, through(j, "uT"))
                            wait(pe, d_a, through(j, "w1"))
                        split3(pe, ps[:, bank, :], hTh[:, s, :], hTl[:, s, :],
                               wqkv_h[:, bass.ds(l, 1), n * INNER:(n + 1) * INNER].rearrange("p o n -> p (o n)"),
                               wqkv_l[:, bass.ds(l, 1), n * INNER:(n + 1) * INNER].rearrange("p o n -> p (o n)")).then_inc(done, 1)
                g, s, live = at(j, u, "hnT")
                if live:
                    wait(pe, d_hn, g + 1)
                    wait(pe, d_x2, through(j, "oT"))
                    pe.transpose(ps[:, 0, 2 * P:3 * P], hn[:, s % 2, :], eye[:, :]).then_inc(p_hnT, 1)
                g, s, live = at(j, u, "pT")
                if live:
                    for b in range(2):
                        wait(pe, a_exp, 2 * g + b + 1)
                        wait(pe, (a_qT, a_kT)[b], through(j, "qkT"))
                        for c in range(HP):
                            last = pe.transpose(ps[:, 4 + b, c * P:(c + 1) * P], pr[:, s % 2, b, c, :], eye[:, :])
                        last.then_inc(p_pT, 1)
                g, s, live = at(j, u, "uT")
                if live:
                    wait(pe, a_uT, g + 1)
                    wait(pe, d_hnTl, through(j, "hnT"))
                    wait(pe, d_x, T + g)
                    l = layer(g)
                    pe.matmul(ps[:, 0, 3 * P:4 * P], ones2[:, :], b2_hl[:, bass.ds(l, 1), :].rearrange("p o n -> p (o n)"),
                              start=True, stop=False)
                    for c in range(HC):
                        last = pe.matmul(ps[:, 0, 3 * P:4 * P], fuT[:, s % 2, c, :],
                                         w2[:, bass.ds(l, 1), c, :].rearrange("p o n -> p (o n)"), start=False, stop=c == HC - 1)
                    last.then_inc(p_w2, 1)
                g, s, live = at(j, u, "pT")
                if live:
                    for b in range(2):
                        if b == 0:
                            wait(pe, a_pT, g + 1)
                            wait(pe, m_v[s], 2 * 16 * (g // R + 1))
                        else:
                            wait(pe, d_pT, g + 1)
                        for c in range(HP):
                            h = 2 * c + b
                            for w, v in enumerate((v_back, v_own)):
                                last = pe.matmul(ps[W * w:W * (w + 1), 4 + b, c * (DH + 1):(c + 1) * (DH + 1)],
                                                 prT[:, b, c, W * w:W * (w + 1)], v[:, s, h, :], start=True, stop=True)
                        last.then_inc(p_pv, 1)

            stream(pe, step)


_LOADS = {"x": "L0_attn_hidden_states", "Wq": "L0_attn_Wq", "bq": "L0_attn_bq", "Wk": "L0_attn_Wk", "bk": "L0_attn_bk",
          "Wv": "L0_attn_Wv", "bv": "L0_attn_bv", "wqkv": "L0_ffn_wqkv", "wo": "L0_ffn_wo", "ln_g": "L0_ffn_ln_g",
          "ln_b": "L0_ffn_ln_b", "w1": "L0_ffn_w1", "b1": "L0_ffn_b1", "w2": "L0_ffn_w2", "b2": "L0_ffn_b2"}


def kernel(**inputs):
    import concourse.bacc as bacc
    from concourse.bass_utils import run_bass_kernel_spmd

    nc = bacc.Bacc("TRN2", target_bir_lowering=False, num_devices=1)
    arrays = {name: np.ascontiguousarray(inputs[key]) for name, key in _LOADS.items()}
    arrays["scales"] = np.concatenate([np.asarray(inputs["L0_ffn_q_scale"]).ravel(), np.asarray(inputs["L0_ffn_k_scale"]).ravel()])
    arrays["ln_g"] = np.ascontiguousarray(arrays["ln_g"].T)
    arrays["ln_b"] = np.ascontiguousarray(np.stack([arrays["ln_b"].T] * 2, axis=-1))
    arrays.update(constants())
    dram = {name: nc.dram_tensor("in_" + name, a.shape, mybir.dt.from_np(a.dtype), kind="ExternalInput").ap()
            for name, a in arrays.items()}
    out = nc.dram_tensor("out", (B, N, D), F32, kind="ExternalOutput").ap()
    build(nc, dram, out)
    return run_bass_kernel_spmd(nc, [{"in_" + n: a for n, a in arrays.items()}], core_ids=[0]).results[0]["out"]
```

```python
from contextlib import ExitStack

import numpy as np

import concourse.bass as bass
from concourse import mybir

F32 = mybir.dt.float32
F32R = mybir.dt.float32r
BF16 = mybir.dt.bfloat16
I32 = mybir.dt.int32
ALU = mybir.AluOpType
ACT = mybir.ActivationFunctionType
AX = mybir.AxisListType

P = 128
B, N, D = 2, 1024, 128
TB = N // P
T = B * TB
DEPTH = 2
H, DH, W = 8, 64, 64
INNER = H * DH
HP = H // 2
HID = int(D * 4 * 2 / 3)
HE = HID + HID % 2
HC = 3
G = T * DEPTH
R = 4
GT = R
NG = T // GT
QK_SCALE = 8.0
A_SCALE = 1.0 / 8.0
EPS = 1e-5
NORM_FLOOR2 = 1e-24
RSQRT_SEED = float(0x5F3759DF - 2 ** 30 - 2 ** 22)
MASKED = -1e30
ARENA = 22592

SKEW = dict(h=0, v=1, qkT=2, pT=3, oT=4, hnT=5, w1=6, u=7, uT=8)
FILL = 12
LAST = G + SKEW["uT"]
HAND_OVER = ((0, 0), (1, 0), (0, 1), (0, 2), (0, 3), (1, 1), (0, 4), (0, 5), (0, 6), (0, 7), (1, 2))


def slot(g):
    return ((g % T) * (TB + 1)) // TB + 1


def slot2(g):
    return g % TB + 1


STEPS_NEWTON = 12
SLOTS = B * (TB + 1)


def constants():
    f = np.float32
    inv = (f(10000.0) ** (np.arange(0, 64, 2, dtype=f) / f(64))).astype(f)
    rad = (np.arange(N, dtype=f)[:, None] / inv).astype(f)
    sincos = np.stack((np.sin(rad), np.cos(rad)), axis=-1).reshape(N, -1)
    rope = np.repeat(sincos, 2, axis=-1).astype(f)
    turn = np.eye(P, dtype=f)
    for i in range(0, P, 2):
        turn[i + 1, i] = -1.0
        turn[i, i + 1] = 1.0
    half = np.arange(0, DH, 2, dtype=f)
    inv_freq = (f(1.0) / f(10000.0) ** (half / f(DH))).astype(f)
    t = np.arange(N, dtype=f)
    freqs = t[:, None] * inv_freq[None, :]
    freqs = np.concatenate([freqs, freqs], axis=-1)
    base = (half + f(0.4 * DH)) / f(1.4 * DH)
    power = (t - N // 2) / f(W // 2)
    scale = (base[None, :] ** power[:, None]).astype(f)
    scale = np.concatenate([scale, scale], axis=-1)
    cos, sin = np.cos(freqs).astype(f), np.sin(freqs).astype(f)
    sign = np.concatenate([-np.ones(DH // 2, f), np.ones(DH // 2, f)])
    tabs = [cos * scale * f(QK_SCALE), sin * scale * sign * f(QK_SCALE), cos / scale, sin / scale * sign]
    xpos = np.stack(tabs).astype(f).reshape(4, TB, P, DH).transpose(2, 0, 1, 3)
    i = (np.arange(P) % W)[:, None]
    r = np.arange(2 * W)[None, :]
    band = (r >= i) & (r <= i + W)
    first = band & ((np.arange(P)[:, None] >= W) | (r >= W))
    mask = np.where(np.stack([first, band], axis=1), 0.0, MASKED).astype(np.float32)
    return {
        "rope": np.ascontiguousarray(rope.T), "turn": turn, "eye": np.eye(P, dtype=f),
        "xpos": np.ascontiguousarray(xpos), "mask": mask,
    }


def build(nc, d, out):
    ctx = ExitStack()
    with ctx:
        def sb(name, shape, dt=F32):
            return ctx.enter_context(nc.sbuf_tensor(name, shape, dt))

        def sem(name):
            return ctx.enter_context(nc.semaphore(name))

        arena = sb("arena", [P, ARENA])
        taken = {"before": 0, "after": 0}

        def place(lot, shape):
            n = int(np.prod(shape[1:]))
            at0 = taken[lot]
            taken[lot] += n + n % 2
            assert taken[lot] <= ARENA, (lot, taken)
            dims = " ".join(f"d{i}" for i in range(len(shape) - 1))
            sizes = {f"d{i}": shape[i + 1] for i in range(1, len(shape) - 1)}
            flat = arena[0:shape[0], at0:at0 + n]
            return flat.rearrange(f"p ({dims}) -> p {dims}", **sizes) if len(shape) > 2 else flat

        def before(name, shape):
            return place("before", shape)

        def after(name, shape):
            return place("after", shape)

        eye = sb("eye", [P, P])
        eye16 = sb("eye16", [P, P], BF16)
        turn = before("turn", [P, P])
        rope = before("rope", [P, N])
        mask32 = before("mask32", [P, 2, 2 * W])
        mask = sb("mask", [P, 2, 4 * 2 * W], BF16)
        xpos = before("xpos", [P, 4, TB, DH])
        scales = before("scales", [P, 2, DEPTH, DH])
        xtab = sb("xtab", [P, 4, DEPTH * TB, DH])
        wa = before("wa", [P, 3, P])
        waT = before("waT", [P, 3, P])
        ba = before("ba", [P, 2])
        baT = before("baT", [P, 2])
        bv = before("bv", [P, P])
        wqkv = before("wqkv", [P, DEPTH, 3 * INNER])
        wqkv_h = sb("wqkv_h", [P, DEPTH, 3 * INNER], F32R)
        wqkv_l = sb("wqkv_l", [P, DEPTH, 3 * INNER], F32R)
        wo = sb("wo", [P, DEPTH, 4, P])
        w1 = before("w1", [P, DEPTH, 2, HE])
        w1g = before("w1g", [P, DEPTH, 2, HE])
        w1_h = sb("w1_h", [P, DEPTH, 2, HE], F32R)
        w1_l = sb("w1_l", [P, DEPTH, 2, HE], F32R)
        lng = before("lng", [P, DEPTH])
        lnb = before("lnb", [P, DEPTH, 2])
        b1 = before("b1", [2, DEPTH, 2, HE])
        b1_hl = sb("b1_hl", [2, DEPTH, 2, HE], F32R)
        w2 = sb("w2", [P, DEPTH, HC, P])
        b2 = before("b2", [2, DEPTH, P])
        b2_hl = sb("b2_hl", [2, DEPTH, P], F32R)
        ones2 = sb("ones2", [2, P], F32R)
        ones2f = before("ones2f", [2, P])
        signs = sb("signs", [2, 1])
        c15 = sb("c15", [P, 2 * H + 1])
        gap = sb("gap", [P, 1])

        x_in = sb("x_in", [P, T, D])
        stats = sb("stats", [P, T, 6])
        mv = sb("mv", [P, T, 2])
        var = sb("var", [P, T])
        rstd = sb("rstd", [P, T])
        newt = sb("newt", [P, T])
        qT32 = before("qT32", [P, T, P])
        kT32 = before("kT32", [P, 2, GT * P])
        kTh = sb("kTh", [P, B, N], F32R)
        kTl = sb("kTl", [P, B, N], F32R)
        kTh_all = kTh[:, :, :].rearrange("p b n -> p (b n)")
        kTl_all = kTl[:, :, :].rearrange("p b n -> p (b n)")
        va = before("va", [P, T, D])
        qh = sb("qh", [P, R, P], F32R)
        ql = sb("ql", [P, R, P], F32R)
        nmax = sb("nmax", [P, 2])
        nbias = sb("nbias", [P, R])
        den = sb("den", [P, R])
        rden = sb("rden", [P, 2])
        pa = before("pa", [P, 2, N])
        paT = before("paT", [P, 2, N])
        xn, xnT = pa[:, :, 0:GT * D], paT[:, :, 0:GT * P]
        x1r = sb("x1r", [P, 2, D])
        x1 = x_in
        mv1 = sb("mv1", [P, R, 2])
        var1 = sb("var1", [P, R])
        rstd1 = sb("rstd1", [P, R])
        newt1 = sb("newt1", [P, GT])

        under = kTh[:, :, :].rearrange("p b n -> p (b n)")
        hTh, hTl, hnTh, hnTl = (under[:, n * 4 * P:(n + 1) * 4 * P].rearrange("p (r n) -> p r n", r=R) for n in range(4))
        oT = after("oT", [P, 2, 4, P])
        qT = after("qT", [P, 2, HP, P])
        xs = sb("xs", [P, SLOTS, D])
        x2s = sb("x2s", [P, 1 + TB, D])
        v_own = after("v_own", [P, R, H, DH + 1])
        kT = after("kT", [P, HP, W + R * P])
        fu = after("fu", [P, R, HC * P])
        h_r = after("h_r", [P, R, D])
        sq = after("sq", [P, 2, INNER])
        t2 = after("t2", [P, 2, INNER])
        qk = after("qk", [P, 2, 2, INNER])
        mm = sb("mm", [P, R, 2 * H + 1])
        yy = sb("yy", [P, R, 2 * H + 1])
        n2, rn = mm[:, :, 0:2 * H], yy[:, :, 0:2 * H]
        newt_n = sb("newt_n", [P, 2 * H + 1])
        v_back = after("v_back", [P, R, H, DH + 1])
        mx = after("mx", [P, R, H])
        nb = after("nb", [P, R, H])
        pr = after("pr", [P, 2, 2, HP, 2 * W])
        prT = after("prT", [P, 2, HP, P])
        ro = after("ro", [P, 2, 2, HP])
        on = after("on", [P, HP, 2, DH])
        h2_r = after("h2_r", [P, R, D])
        st2 = sb("st2", [P, 2, 6])
        mv2 = sb("mv2", [P, R, 2])
        hn = after("hn", [P, 2, D])
        fa = after("fa", [P, R, HE])
        fg = after("fg", [P, R, HE])
        fuT = after("fuT", [P, 2, HC, P])

        ps = ctx.enter_context(nc.psum_tensor("ps", [P, 8, 512], F32))

        s_x = [sem(f"s_x{b}") for b in range(B)]
        s_eye = sem("s_eye")
        s_cst = sem("s_cst")
        s_wa = sem("s_wa")
        s_wl = sem("s_wl")
        s_zero = sem("s_zero")
        s_wprep_act = sem("s_wprep_act")
        s_wprep = sem("s_wprep")
        s_wpe = sem("s_wpe")
        s_xtab = sem("s_xtab")
        s_brow = sem("s_brow")
        s_pads = sem("s_pads")
        s_stat = sem("s_stat")
        s_newt0 = sem("s_newt0")
        s_gprep = sem("s_gprep")
        s_var = sem("s_var")
        s_rstd = sem("s_rstd")
        s_xn = sem("s_xn")
        s_axT = sem("s_axT")
        s_axTs = sem("s_axTs")
        s_apk = sem("s_apk")
        s_apq = sem("s_apq")
        s_apv_own = sem("s_apv_own")
        s_ava = sem("s_ava")
        s_aq = sem("s_aq")
        s_ak32 = sem("s_ak32")
        s_ak = sem("s_ak")
        s_akh = sem("s_akh")
        s_aqh = sem("s_aqh")
        s_aql = sem("s_aql")
        s_asc = sem("s_asc")
        s_amx = sem("s_amx")
        s_anb = sem("s_anb")
        s_aex = sem("s_aex")
        s_apT = sem("s_apT")
        s_apTa = sem("s_apTa")
        s_apv = sem("s_apv")
        s_ard = sem("s_ard")
        s_ax1 = sem("s_ax1")
        s_ast = sem("s_ast")
        s_amv = sem("s_amv")
        s_aeps = sem("s_aeps")
        s_var1 = sem("s_var1")
        s_newt1 = sem("s_newt1")
        s_x1r = sem("s_x1r")
        p_hT, p_q, p_k, p_v = sem("p_hT"), sem("p_q"), sem("p_k"), sem("p_v")
        p_qT, p_kT, p_sc, p_pT, p_pv = sem("p_qT"), sem("p_kT"), sem("p_sc"), sem("p_pT"), sem("p_pv")
        p_oT, p_wo, p_hnT, p_w1, p_uT, p_w2 = (sem(f"p_{n}") for n in ("oT", "wo", "hnT", "w1", "uT", "w2"))
        a_hTh, a_v, a_sq, a_qT, a_kT, a_exp = (sem(f"a_{n}") for n in ("hTh", "v", "sq", "qT", "kT", "exp"))
        a_pT, a_oT, a_hnTh, a_g, a_ge, a_uT = (sem(f"a_{n}") for n in ("pT", "oT", "hnTh", "g", "ge", "uT"))
        d_x, d_hTl, d_t, d_n2, d_nb, d_pT, d_on = (sem(f"d_{n}") for n in ("x", "hTl", "t", "n2", "nb", "pT", "on"))
        d_x2, d_var2, d_hn, d_hnTl, d_a, d_u = (sem(f"d_{n}") for n in ("x2", "var2", "hn", "hnTl", "a", "u"))
        d_ns, d_nc, d_mx, d_ro, d_st2, d_mv2, d_eps2 = (sem(f"d_{n}") for n in ("ns", "nc", "mx", "ro", "st2", "mv2", "eps2"))
        s_newtn = sem("s_newtn")
        s_newt2 = sem("s_newt2")
        g_kadd = sem("g_kadd")
        g_q, g_rn, g_k, g_rstd2 = (sem(f"g_{n}") for n in ("q", "rn", "k", "rstd2"))
        m_h = [sem(f"m_h{i}") for i in range(R)]
        m_v = [sem(f"m_v{i}") for i in range(R)]
        m_h2 = [sem(f"m_h2{i}") for i in range(R)]
        s_ready = sem("s_ready")
        s_turn = sem("s_turn")
        s_y = sem("s_y")
        s_out = sem("s_out")

        NLOAD_EYE, NLOAD_CST, NLOAD_WA, NLOAD_WL = 2, 4, 6, 16

        block = ctx.enter_context(nc.Block())

        def wait(eng, s, v):
            if not (isinstance(v, int) and v <= 0):
                eng.wait_ge(s, v)

        def split3(eng, o, hi, lo, wh, wl, start=True, stop=True):
            eng.matmul(o, hi, wh, start=start, stop=False)
            eng.matmul(o, hi, wl, start=False, stop=False)
            return eng.matmul(o, lo, wh, start=False, stop=stop)

        def pipeline(eng, step, tiles, first, fill):
            for j in range(first, fill):
                step(j, j % R)
            with eng.Fori(fill // R, tiles // R) as i:
                for u in range(R):
                    step(i * R + u, u)

        def attend(eng, step):
            pipeline(eng, step, T, 0, 2 * GT)

        def stream(eng, step, first):
            pipeline(eng, step, G, first, FILL)
            for j in range(G, LAST):
                step(j, j % R)

        def hand_over(eng, astep, step):
            for streams, j in HAND_OVER:
                if streams:
                    step(j, j % R)
                elif astep:
                    astep(T + j, (T + j) % R)
            return max(j for streams, j in HAND_OVER if streams) + 1

        def has(j, skew, tiles=T):
            return not isinstance(j, int) or 0 <= j - skew < tiles

        def newton(gp, y, m, tmp, links, g):
            k = STEPS_NEWTON * g
            for n in range(3):
                gp.tensor_tensor(tmp, y, y, ALU.mult).then_inc(links, 1)
                gp.wait_ge(links, k + 4 * n + 1)
                gp.tensor_tensor(tmp, tmp, m, ALU.mult).then_inc(links, 1)
                gp.wait_ge(links, k + 4 * n + 2)
                gp.tensor_tensor(tmp, tmp, c15[:, 0:tmp.shape[1]], ALU.add).then_inc(links, 1)
                gp.wait_ge(links, k + 4 * n + 3)
                gp.tensor_tensor(y, y, tmp, ALU.mult).then_inc(links, 1)
                gp.wait_ge(links, k + 4 * n + 4)

        def at(j, u, stage):
            k = SKEW[stage]
            live = not isinstance(j, int) or 0 <= j - k < G
            return j - k, (u - k) % R, live

        def through(j, stage):
            n = j - SKEW[stage] + 1
            return min(n, G) if isinstance(j, int) else n

        held = {}

        def index(eng, name, of, j, u, stage, top):
            k = SKEW[stage]
            if isinstance(j, int):
                return of(j - k)
            within = (u - k) % R
            if u == 0 or within == 0:
                reg = held.get((eng.engine, name)) or eng.alloc_register(f"r_{name}")
                eng.reg_mov(reg, of(j - k - within))
                held[eng.engine, name] = reg
                held[eng.engine, name, "value"] = eng.snap(reg, min_val=0, max_val=top)
            return held[eng.engine, name, "value"] + within

        def ahead(eng, name, v, top):
            if isinstance(v, int):
                return v
            if (eng.engine, name) not in held:
                held[eng.engine, name] = eng.alloc_register(f"r_{name}")
            eng.reg_mov(held[eng.engine, name], v)
            return eng.snap(held[eng.engine, name], min_val=0, max_val=top)

        def group_banks(g):
            return (4, 5, 6) if g % 2 == 0 else (7, 0, 1)

        def layer(g):
            return g // T

        def table_row(g):
            return (g // T) * TB + g % TB

        def halves(ap):
            return ap.rearrange("p (h a c) -> p h a c", h=H, a=2)

        @block.sync
        def _(sp):
            sp.dma_start(x_in[:, 0:TB, :], d["x"][0].rearrange("(t p) d -> p t d", p=P)).then_inc(s_x[0], 16)
            sp.dma_start(eye[:, :], d["eye"]).then_inc(s_eye, 16)
            sp.dma_start(turn[:, :], d["turn"]).then_inc(s_eye, 16)
            sp.dma_start(wa[:, 0, :], d["Wq"]).then_inc(s_wa, 16)
            sp.dma_start(wa[:, 1, :], d["Wk"]).then_inc(s_wa, 16)
            sp.dma_start(wa[:, 2, :], d["Wv"]).then_inc(s_wa, 16)
            sp.dma_start(ba[:, 0:1], d["bq"].rearrange("(p a) -> p a", a=1)).then_inc(s_wa, 16)
            sp.dma_start(ba[:, 1:2], d["bk"].rearrange("(p a) -> p a", a=1)).then_inc(s_wa, 16)
            sp.dma_start(x_in[:, TB:T, :], d["x"][1].rearrange("(t p) d -> p t d", p=P)).then_inc(s_x[1], 16)
            sp.dma_start(bv[:, :], d["bv"].partition_broadcast(P)).then_inc(s_wa, 16)
            sp.dma_start(rope[:, :], d["rope"]).then_inc(s_cst, 16)
            sp.dma_start(mask32[:, :, :], d["mask"]).then_inc(s_cst, 16)
            sp.dma_start(xpos[:, :, :, :], d["xpos"]).then_inc(s_cst, 16)
            sp.dma_start(scales[:, :, :, :].rearrange("p a l c -> p (a l c)"),
                         d["scales"].partition_broadcast(P)).then_inc(s_cst, 16)
            sp.wait_ge(s_pads, 3)
            sp.dma_start(wqkv[:, :, :], d["wqkv"].rearrange("l k n -> k l n")).then_inc(s_wl, 16)
            sp.dma_start(wo[:, :, :, :], d["wo"].rearrange("l (c k) n -> k l c n", k=P)).then_inc(s_wl, 16)
            sp.dma_start(lng[:, :], d["ln_g"]).then_inc(s_wl, 16)
            sp.dma_start(lnb[:, :, :], d["ln_b"]).then_inc(s_wl, 16)
            for l in range(DEPTH):
                sp.dma_start(w1[:, l, :, 0:HID], d["w1"][l].rearrange("k (a n) -> k a n", a=2)).then_inc(s_wl, 16)
                sp.dma_start(w2[:, l, 0:2, :], d["w2"][l, 0:2 * P, :].rearrange("(c k) n -> k c n", k=P)).then_inc(s_wl, 16)
                sp.dma_start(w2[0:HID - 2 * P, l, 2, :], d["w2"][l, 2 * P:HID, :]).then_inc(s_wl, 16)
                for r in range(2):
                    sp.dma_start(b1[r:r + 1, l, :, 0:HID], d["b1"][l:l + 1].rearrange("l (a n) -> l a n", a=2)).then_inc(s_wl, 16)
            for r in range(2):
                sp.dma_start(b2[r:r + 1, :, :], d["b2"].rearrange("(a l) n -> a l n", a=1)).then_inc(s_wl, 16)

            def carried(s, v):
                wait(sp, s, v)
                if not isinstance(v, int):
                    sp.sem_inc(s_turn, 1)

            def step(j, u):
                g, s, live = at(j, u, "h")
                if live:
                    before_sl = index(sp, "before", lambda g: slot(g) - 1, j, u, "h", SLOTS - R - 1)
                    sl = before_sl + 1
                    carried(d_x, g + 1)
                    carried(p_hT, g - R + 1)
                    sp.dma_start(h_r[:, s, 0:D // 2], xs[:, sl, 0:D // 2]).then_inc(m_h[s], 16)
                    sp.dma_start(h_r[1:P, s, D // 2:D], xs[0:P - 1, sl, D // 2:D]).then_inc(m_h[s], 16)
                    sp.dma_start(h_r[0:1, s, D // 2:D], xs[P - 1:P, before_sl, D // 2:D]).then_inc(m_h[s], 16)
                g, s, live = at(j, u, "v")
                if live:
                    carried(a_v, g + 1)
                    carried(p_pv, 2 * (g - R + 1))
                    sp.dma_start(v_back[0:W, s, :, :], v_own[W:P, (s - 1) % R, :, :]).then_inc(m_v[s], 16)
                    sp.dma_start(v_back[W:P, s, :, :], v_own[0:W, s, :, :]).then_inc(m_v[s], 16)
                g, s, live = at(j, u, "oT")
                if live:
                    before_sl = index(sp, "before2", lambda g: slot2(g) - 1, j, u, "oT", TB - R)
                    sl = before_sl + 1
                    carried(d_x2, g + 1)
                    carried(d_hn, g - R + 1)
                    sp.dma_start(h2_r[:, s, 0:D // 2], x2s[:, sl, 0:D // 2]).then_inc(m_h2[s], 16)
                    sp.dma_start(h2_r[1:P, s, D // 2:D], x2s[0:P - 1, sl, D // 2:D]).then_inc(m_h2[s], 16)
                    sp.dma_start(h2_r[0:1, s, D // 2:D], x2s[P - 1:P, before_sl, D // 2:D]).then_inc(m_h2[s], 16)

            sp.wait_ge(s_zero, 4)
            sp.wait_ge(s_ready, 3)
            stream(sp, step, 0)
            o = out.rearrange("b (t p) d -> p (b t) d", p=P)
            sp.wait_ge(s_y, 1)
            sp.dma_start(o[:, 0:T // 2, :], x1[:, 0:T // 2, :]).then_inc(s_out, 16)
            for t in range(T // 2, T):
                sp.wait_ge(s_y, 2 + t - T // 2)
                sp.dma_start(o[:, t, :], x1[:, t, :]).then_inc(s_out, 16)
            sp.wait_ge(s_out, 16 * (1 + T // 2))

        @block.gpsimd
        def _(gp):
            for t in (w1, w2, b1):
                gp.memset(t[:], 0.0).then_inc(s_pads, 1)
            gp.memset(ones2f[:], 1.0).then_inc(s_zero, 1)
            gp.memset(c15[:], 1.5).then_inc(s_zero, 1)
            gp.memset(xs[:].rearrange("p (b t) d -> p b t d", t=TB + 1)[:, :, 0, :], 0.0).then_inc(s_zero, 1)
            gp.memset(x2s[:, 0, :], 0.0).then_inc(s_zero, 1)
            gp.wait_ge(s_zero, 4)
            for b in range(B):
                gp.wait_ge(s_var, b + 1)
                newton(gp, rstd[:, b * TB:(b + 1) * TB], var[:, b * TB:(b + 1) * TB], newt[:, 0:TB], s_newt0, b)
            gp.wait_ge(s_wl, 16 * NLOAD_WL)
            for l in range(DEPTH):
                gp.tensor_scalar(w1g[:, l], w1[:, l], lng[:, l:l + 1], 1.0, ALU.mult, ALU.mult).then_inc(s_gprep, 1)
            for g in range(NG):
                gp.wait_ge(s_akh, g + 1)
                cols = slice(g * GT * P, (g + 1) * GT * P)
                gp.tensor_tensor(kTl_all[:, cols], kT32[:, g % 2, :], kTh_all[:, cols].bitcast(F32), ALU.subtract).then_inc(s_ak, 1)
            gp.wait_ge(s_wprep_act, 5)
            gp.tensor_tensor(wqkv_l[:], wqkv[:], wqkv_h[:].bitcast(F32), ALU.subtract)
            gp.wait_ge(s_wprep_act, 6)
            gp.tensor_tensor(w1_l[:], w1g[:], w1_h[:].bitcast(F32), ALU.subtract).then_inc(s_gprep, 1)
            def second_rstd(n):
                gp.wait_ge(s_var1, n + 1)
                newton(gp, rstd1[:, :], var1[:, :], newt1[:, :], s_newt1, n)

            gp.wait_ge(s_cst, 16 * NLOAD_CST)
            for n in range(2):
                gp.tensor_copy(mask[:, n, :].rearrange("p (c r) -> p c r", c=HP),
                               mask32[:, n, :].unsqueeze(1).to_broadcast([P, HP, 2 * W]))
            gp.tensor_copy(eye16[:, :], eye[:, :])
            second_rstd(0)
            for a in range(2):
                for l in range(DEPTH):
                    own = scales[:, a, l, :].rearrange("p (b c) -> p b c", b=2)
                    for k, sc in ((2 * a, own), (2 * a + 1, own[:, ::-1, :])):
                        last = gp.tensor_tensor(xtab[:, k, l * TB:(l + 1) * TB, :].rearrange("p t (b c) -> p t b c", b=2),
                                                xpos[:, k, :, :].rearrange("p t (b c) -> p t b c", b=2),
                                                sc.unsqueeze(1).to_broadcast([P, TB, 2, DH // 2]), ALU.mult)
            last.then_inc(s_xtab, 1)
            gp.wait_ge(s_xtab, 1)
            gp.wait_ge(s_aq, NG)
            gp.wait_ge(s_ava, NG)
            gp.wait_ge(s_wprep_act, 6)
            gp.memset(v_own[:], 1.0).then_inc(s_ready, 1)
            gp.memset(kT[:, :, 0:W], 0.0).then_inc(s_ready, 1)
            gp.memset(fu[:, :, HE:HC * P], 0.0).then_inc(s_ready, 1)
            for n in range(1, T // GT - 1):
                second_rstd(n)

            def astep(j, u):
                if j == T + GT - 1:
                    second_rstd(T // GT - 1)

            def step(j, u):
                g, s, live = at(j, u, "h")
                if live:
                    r = s % 2
                    wait(gp, d_t, 2 * g + 1)
                    gp.tensor_tensor(qk[:, r, 1, :], qk[:, r, 1, :], t2[:, 1, :], ALU.add).then_inc(g_kadd, 1)
                    wait(gp, d_t, 2 * g + 2)
                    gp.tensor_tensor(qk[:, r, 0, :], qk[:, r, 0, :], t2[:, 0, :], ALU.add).then_inc(g_q, 1)
                _, _, normed = at(j, u, "oT")
                if live or normed:
                    c = slice(0 if live else 2 * H, 2 * H + 1 if normed else 2 * H)
                    if live:
                        wait(gp, d_n2, g + 1)
                    if normed:
                        wait(gp, d_var2, through(j, "oT"))
                    newton(gp, yy[:, u, c], mm[:, u, c], newt_n[:, c], s_newtn, j)
                if live:
                    wait(gp, g_kadd, g + 1)
                    gp.tensor_tensor(qk[:, r, 1, :].rearrange("p (h c) -> p h c", h=H),
                                     qk[:, r, 1, :].rearrange("p (h c) -> p h c", h=H),
                                     rn[:, s, H:2 * H].unsqueeze(2).to_broadcast([P, H, DH]), ALU.mult).then_inc(g_k, 1)

            stream(gp, step, hand_over(gp, astep, step))

        @block.scalar
        def _(act):
            act.wait_ge(s_wpe, 1)
            act.activation(waT[:, :, :], ps[:, 0, 0:3 * P].rearrange("p (a n) -> p a n", a=3), ACT.Copy).then_inc(s_wprep_act, 1)
            act.activation(baT[:, :], ps[:, 0, 3 * P:3 * P + 2], ACT.Copy).then_inc(s_wprep_act, 1)

            for n in range(NG + 1):
                if n < NG:
                    act.wait_ge(s_axT, n + 1)
                    wait(act, s_apv_own, n - 1)
                    act.activation(xnT[:, n % 2, :], ps[:, 2 + n % 2, :], ACT.Copy).then_inc(s_axTs, 1)
                if n >= 1:
                    g = n - 1
                    act.wait_ge(s_ak32, g + 1)
                    act.activation(kTh_all[:, g * GT * P:(g + 1) * GT * P], kT32[:, g % 2, :], ACT.Copy).then_inc(s_akh, 1)
                if n == 1:
                    act.wait_ge(s_wl, 16 * NLOAD_WL)
                    act.wait_ge(s_zero, 1)
                    act.activation(ones2[:], ones2f[:], ACT.Copy).then_inc(s_wprep_act, 1)
                    act.activation(wqkv_h[:, 0], wqkv[:, 0], ACT.Copy).then_inc(s_wprep_act, 1)
                if n == 2:
                    act.activation(wqkv_h[:, 1], wqkv[:, 1], ACT.Copy).then_inc(s_wprep_act, 1)
                if n == 3:
                    act.wait_ge(s_gprep, DEPTH)
                    act.activation(w1_h[:], w1g[:], ACT.Copy).then_inc(s_wprep_act, 1)

            def astep(j, u):
                if isinstance(j, int) and j == 3:
                    act.wait_ge(s_wprep, 1)
                    for k, (bias, parts) in enumerate(((b1, b1_hl), (b2, b2_hl))):
                        act.activation(parts[:], bias[:], ACT.Copy).then_inc(s_brow, 1)
                        act.wait_ge(s_brow, 2 * k + 1)
                        act.activation(bias[:], bias[:], ACT.Copy, scale=eye[0:2, 1:2]).then_inc(s_brow, 1)
                if has(j, 2):
                    g, s = j - 2, (u - 2) % 2
                    wait(act, s_apT, g + 1)
                    wait(act, s_apv, g - 1)
                    act.activation(paT[:, s, :].rearrange("p (a n) -> p a n", a=2), ps[:, 4:6, :], ACT.Copy).then_inc(s_apTa, 1)
                if has(j, 1):
                    g, s = j - 1, (u - 1) % R
                    b = 2 * (s % 2)
                    wait(act, s_anb, g + 1)
                    wait(act, s_apT, g - 1)
                    act.activation(pa[:, s % 2, :].rearrange("p (a n) -> p a n", a=2), ps[:, b:b + 2, :], ACT.Exp,
                                   bias=nbias[:, s:s + 1], scale=A_SCALE, accum_out=den[:, s:s + 1]).then_inc(s_aex, 1)

            attend(act, astep)
            act.wait_ge(s_ready, 3)

            def exponentials(g, s, b):
                wait(act, d_nb, 2 * g + b + 1)
                for c in range(HP):
                    h = 2 * c + b
                    last = act.activation(pr[:, s % 2, b, c, :], ps[:, 6 + b, c * P:(c + 1) * P], ACT.Exp,
                                          bias=nb[:, s, b * HP + c:b * HP + c + 1], scale=rn[:, s, h:h + 1])
                last.then_inc(a_exp, 1)

            def step(j, u):
                g, s, live = at(j, u, "qkT")
                if live:
                    wait(act, p_kT, g + 1)
                    k_ps = ps[:, 5, :].rearrange("p (c n) -> p c n", c=HP)
                    last = act.activation(kT[:, :, W + s * P:W + (s + 1) * P], k_ps, ACT.Copy)
                    if s == R - 1:
                        last = act.activation(kT[:, :, 0:W], k_ps[:, :, W:P], ACT.Copy)
                    last.then_inc(a_kT, 1)
                g, s, live = at(j, u, "qkT")
                if live:
                    wait(act, p_qT, g + 1)
                    act.activation(qT[:, s % 2, :, :], ps[:, 4, :].rearrange("p (c n) -> p c n", c=HP), ACT.Copy).then_inc(a_qT, 1)
                g, s, live = at(j, u, "w1")
                if live:
                    wait(act, p_w1, g + 1)
                    wait(act, d_u, (g - 2) // 2)
                    act.activation(fg[:, s, :], ps[:, 2, 0:HE], ACT.Copy).then_inc(a_g, 1)
                g, s, live = at(j, u, "h")
                if live:
                    wait(act, p_hT, g + 1)
                    act.activation(hTh[:, s, :], ps[:, 0, 0:P], ACT.Copy).then_inc(a_hTh, 1)
                g, s, live = at(j, u, "oT")
                if live:
                    wait(act, p_oT, g + 1)
                    wait(act, p_wo, g - 1)
                    act.activation(oT[:, s % 2], ps[:, 3, :].rearrange("p (c n) -> p c n", c=4), ACT.Copy).then_inc(a_oT, 1)
                g, s, live = at(j, u, "qkT")
                if live:
                    exponentials(g, s, 0)
                g, s, live = at(j, u, "uT")
                if live:
                    wait(act, p_uT, g + 1)
                    act.activation(fuT[:, s % 2, :, :], ps[:, 1, 0:HC * P].rearrange("p (c n) -> p c n", c=HC), ACT.Copy).then_inc(a_uT, 1)
                g, s, live = at(j, u, "qkT")
                if live:
                    exponentials(g, s, 1)
                g, s, live = at(j, u, "pT")
                if live:
                    wait(act, p_pT, 2 * g + 1)
                    act.activation(prT[:, 0, :, :], ps[:, 4, :].rearrange("p (c n) -> p c n", c=HP), ACT.Copy).then_inc(a_pT, 1)
                g, s, live = at(j, u, "hnT")
                if live:
                    wait(act, p_hnT, g + 1)
                    act.activation(hnTh[:, s, :], ps[:, 0, 2 * P:3 * P], ACT.Copy).then_inc(a_hnTh, 1)
                g, s, live = at(j, u, "u")
                if live and s % 2 == 0:
                    wait(act, a_g, g + 2)
                    act.activation(fg[:, s:s + 2, :], fg[:, s:s + 2, :], ACT.Gelu).then_inc(a_ge, 1)
                g, s, live = at(j, u, "h")
                if live:
                    wait(act, p_v, g + 1)
                    wait(act, p_pv, 2 * (g - R + 1))
                    if not isinstance(g, int) or g >= R:
                        wait(act, m_v[(s + 1) % R], 2 * 16 * ((g - R + 1) // R + 1))
                    act.activation(v_own[:, s, :, 0:DH], ps[:, 3, :].rearrange("p (h c) -> p h c", h=H), ACT.Copy).then_inc(a_v, 1)
                g, s, live = at(j, u, "h")
                if live:
                    wait(act, d_n2, g)
                    wait(act, d_t, 2 * g + 1)
                    act.activation(sq[:, 1, :], ps[:, 2, :], ACT.Square).then_inc(a_sq, 1)
                g, s, live = at(j, u, "h")
                if live:
                    wait(act, d_t, 2 * g + 2)
                    act.activation(sq[:, 0, :], ps[:, 1, :], ACT.Square).then_inc(a_sq, 1)

            stream(act, step, hand_over(act, astep, step))

        @block.vector
        def _(dve):
            def seed(y, x):
                return dve.tensor_scalar(y.bitcast(I32), x.bitcast(I32), -0.5, RSQRT_SEED, ALU.mult, ALU.add)

            done = 0
            for b in range(B):
                tiles = range(b * TB, (b + 1) * TB)
                dve.wait_ge(s_x[b], 16)
                for t in tiles:
                    dve.bn_stats(stats[:, t, :], x_in[:, t, :]).then_inc(s_stat, 1)
                for t in tiles:
                    done += 1
                    dve.wait_ge(s_stat, done)
                    dve.bn_aggr(mv[:, t, :], stats[:, t, :]).then_inc(s_stat, 1)
                done += TB
                rows = slice(b * TB, (b + 1) * TB)
                dve.wait_ge(s_stat, done)
                dve.tensor_scalar(var[:, rows], mv[:, rows, 1], EPS, -0.5, ALU.add, ALU.mult).then_inc(s_stat, 1)
                done += 1
                dve.wait_ge(s_stat, done)
                seed(rstd[:, rows], var[:, rows]).then_inc(s_var, 1)

            def normalise(n):
                dve.wait_ge(s_newt0, STEPS_NEWTON * (n * GT // TB + 1))
                wait(dve, s_axT, n - 1)
                for k in range(GT):
                    t = n * GT + k
                    last = dve.tensor_scalar(xn[:, n % 2, k * D:(k + 1) * D], x_in[:, t, :], mv[:, t, 0:1], rstd[:, t:t + 1],
                                             ALU.subtract, ALU.mult)
                last.then_inc(s_xn, 1)

            normalise(0)
            normalise(1)
            dve.wait_ge(s_cst, 16 * NLOAD_CST)
            dve.wait_ge(s_wa, 16 * NLOAD_WA)
            dve.wait_ge(s_wprep_act, 2)
            for n in range(2, NG + 2):
                if n < NG:
                    normalise(n)
                g = n - 2
                k_ps, q_ps, v_ps = (ps[:, bank, :] for bank in group_banks(g))
                r = rope[:, (g * GT % TB) * P:(g * GT % TB + GT) * P]
                dve.wait_ge(s_apk, g + 1)
                wait(dve, s_ak, g - 1)
                dve.scalar_tensor_tensor(kT32[:, g % 2, :], k_ps, baT[:, 1:2], r, ALU.add, ALU.mult).then_inc(s_ak32, 1)
                dve.wait_ge(s_apq, g + 1)
                dve.scalar_tensor_tensor(qT32[:, g * GT:(g + 1) * GT, :].rearrange("p a n -> p (a n)"), q_ps, baT[:, 0:1], r,
                                         ALU.add, ALU.mult).then_inc(s_aq, 1)
                dve.wait_ge(s_apv_own, g + 1)
                dve.tensor_tensor(va[:, g * GT:(g + 1) * GT, :], v_ps.rearrange("p (a n) -> p a n", a=GT),
                                  bv[:, :].unsqueeze(1).to_broadcast([P, GT, D]), ALU.add).then_inc(s_ava, 1)

            dve.tensor_tensor(signs[:, :], eye[0:2, 0:1], eye[0:2, 1:2], ALU.subtract)
            dve.wait_ge(s_zero, 4)

            def biases(k):
                if k == 0:
                    dve.wait_ge(s_wpe, 2)
                    dve.tensor_tensor(b1[:].rearrange("p l a n -> p (l a) n"), b1[:].rearrange("p l a n -> p (l a) n"),
                                      ps[0:2, 4:8, 0:HE], ALU.add).then_inc(s_wprep, 1)
                for bias, parts, flat in ((b1, b1_hl, "p l a n -> p (l a n)"), (b2, b2_hl, "p l n -> p (l n)"))[k - 1:k] if k else ():
                    dve.wait_ge(s_brow, 2 * k)
                    dve.scalar_tensor_tensor(parts[:].rearrange(flat), parts[:].bitcast(F32).rearrange(flat), signs[:, :],
                                             bias[:].rearrange(flat), ALU.mult, ALU.add).then_inc(s_wprep, 1)

            dve.wait_ge(s_aq, NG)

            def astep(j, u):
                if has(j, 0):
                    q = qT32[:, bass.ds(j, 1), :].rearrange("p a n -> p (a n)")
                    wait(dve, s_asc, j - R + 1)
                    dve.tensor_scalar(qh[:, u, :], q, 1.0, None, ALU.mult).then_inc(s_aqh, 1)
                    wait(dve, s_aqh, j + 1)
                    dve.tensor_tensor(ql[:, u, :], q, qh[:, u, :].bitcast(F32), ALU.subtract).then_inc(s_aql, 1)
                if has(j, 1):
                    g, s = j - 1, (u - 1) % R
                    b = 2 * (s % 2)
                    wait(dve, s_asc, g + 1)
                    dve.tensor_reduce(out=nmax[:, s % 2:s % 2 + 1], in_=ps[:, b:b + 2, :], axis=AX.XY, op=ALU.max,
                                      negate=True).then_inc(s_amx, 1)
                    wait(dve, s_amx, g + 1)
                    dve.tensor_scalar(nbias[:, s:s + 1], nmax[:, s % 2:s % 2 + 1], A_SCALE, None, ALU.mult).then_inc(s_anb, 1)
                if isinstance(j, int) and j in (1, 4, 5):
                    biases((1, 4, 5).index(j))
                if has(j, 2 * GT):
                    g = j - 2 * GT
                    wait(dve, s_x1r, g + 1)
                    wait(dve, s_newt1, STEPS_NEWTON * (g // GT + 1))
                    dve.tensor_scalar(xs[:, bass.ds(slot(g), 1), :].rearrange("p a n -> p (a n)"),
                                      x1[:, bass.ds(g, 1), :].rearrange("p a n -> p (a n)"),
                                      mv1[:, u, 0:1], rstd1[:, u:u + 1], ALU.subtract, ALU.mult).then_inc(d_x, 1)
                if has(j, 4):
                    g, s = j - 4, (u - 4) % R
                    x1g = x1r[:, s % 2, :]
                    wait(dve, s_apv, g + 1)
                    dve.reciprocal(rden[:, s % 2:s % 2 + 1], den[:, s:s + 1]).then_inc(s_ard, 1)
                    wait(dve, s_ard, g + 1)
                    dve.scalar_tensor_tensor(x1g, ps[:, 6 + s % 2, 0:P], rden[:, s % 2:s % 2 + 1],
                                             x_in[:, bass.ds(g, 1), :].rearrange("p a n -> p (a n)"),
                                             ALU.mult, ALU.add).then_inc(s_ax1, 1)
                    wait(dve, s_ax1, g + 1)
                    dve.bn_stats(stats[:, s, :], x1g).then_inc(s_ast, 1)
                    wait(dve, s_ast, g + 1)
                    dve.memset(gap[:, :], 0.0)
                    dve.bn_aggr(mv1[:, s, :], stats[:, s, :]).then_inc(s_amv, 1)
                    dve.tensor_scalar(x1[:, bass.ds(g, 1), :].rearrange("p a n -> p (a n)"), x1g, 1.0, None, ALU.mult).then_inc(s_x1r, 1)
                    if s == R - 1:
                        wait(dve, s_amv, g + 1)
                        dve.tensor_scalar(var1[:, :], mv1[:, :, 1], EPS, -0.5, ALU.add, ALU.mult).then_inc(s_aeps, 1)
                        wait(dve, s_aeps, (g + 1) // GT)
                        seed(rstd1[:, :], var1[:, :]).then_inc(s_var1, 1)

            attend(dve, astep)
            dve.wait_ge(s_xtab, 1)
            dve.wait_ge(s_ready, 3)

            def tile_of(t, i):
                return t[:, bass.ds(i, 1), :].rearrange("p a n -> p (a n)")

            def products(g, u, row, a, ready, bank):
                r = u % 2
                wait(dve, ready, g + 1)
                wait(dve, (g_q, g_kadd)[a], g)
                dve.tensor_tensor(qk[:, r, a, :].rearrange("p (h c) -> p h c", h=H),
                                  ps[:, bank, :].rearrange("p (h c) -> p h c", h=H),
                                  xtab[:, 2 * a, bass.ds(row, 1), :].to_broadcast([P, H, DH]), ALU.mult)
                dve.tensor_tensor(halves(t2[:, a, :]), halves(ps[:, bank, :])[:, :, ::-1, :],
                                  xtab[:, 2 * a + 1, bass.ds(row, 1), :].rearrange("p o (b c) -> p o b c", b=2)
                                  .to_broadcast([P, H, 2, DH // 2]), ALU.mult).then_inc(d_t, 1)

            def sums_of(b):
                return ps[:, 4 + b, 0:HP * (DH + 1)].rearrange("p (c n) -> p c n", c=HP)

            def maxima(g, s, b):
                wait(dve, p_sc, 2 * g + b + 1)
                dve.tensor_reduce(out=mx[:, s, b * HP:(b + 1) * HP], in_=ps[:, 6 + b, :].rearrange("p (c n) -> p c n", c=HP),
                                  axis=AX.X, op=ALU.max).then_inc(d_mx, 1)

            def minus_maxima(g, s, b):
                wait(dve, d_mx, 2 * g + b + 1)
                dve.scalar_tensor_tensor(nb[:, s, b * HP:(b + 1) * HP], mx[:, s, b * HP:(b + 1) * HP], -1.0,
                                         rn[:, s, b:H:2], ALU.mult, ALU.mult).then_inc(d_nb, 1)

            def step(j, u):
                row = index(dve, "row", table_row, j, u, "h", DEPTH * TB - R)
                wo_slot, w2_slot = (index(dve, "slot_" + stage, slot, j, u, stage, SLOTS - R) for stage in ("oT", "uT"))
                wo_slot2, w2_slot2 = (index(dve, "slot2_" + stage, slot2, j, u, stage, TB - R + 1) for stage in ("oT", "uT"))
                g, s, live = at(j, u, "w1")
                if live:
                    wait(dve, p_w1, g + 1)
                    wait(dve, d_u, (g - 2) // 2)
                    dve.tensor_copy(fa[:, s, :], ps[:, 1, 0:HE]).then_inc(d_a, 1)
                g, s, live = at(j, u, "h")
                if live:
                    wait(dve, a_hTh, g + 1)
                    dve.tensor_tensor(hTl[:, s, :], ps[:, 0, 0:P], hTh[:, s, :].bitcast(F32), ALU.subtract).then_inc(d_hTl, 1)
                g, s, live = at(j, u, "qkT")
                if live:
                    maxima(g, s, 0)
                g, s, live = at(j, u, "qkT")
                if live:
                    minus_maxima(g, s, 0)
                g, s, live = at(j, u, "qkT")
                if live:
                    maxima(g, s, 1)
                g, s, live = at(j, u, "qkT")
                if live:
                    minus_maxima(g, s, 1)
                g, s, live = at(j, u, "oT")
                if live:
                    wait(dve, p_wo, g + 1)
                    dve.tensor_tensor(tile_of(x2s, wo_slot2), ps[:, 0, P:2 * P], tile_of(xs, wo_slot), ALU.add).then_inc(d_x2, 1)
                g, s, live = at(j, u, "hnT")
                if live:
                    wait(dve, s_newtn, STEPS_NEWTON * (g + SKEW["oT"] + 1))
                    dve.tensor_scalar(hn[:, s % 2, :], h2_r[:, s, :], mv2[:, s, 0:1], yy[:, (u - 1) % R, 2 * H:2 * H + 1],
                                      ALU.subtract, ALU.mult).then_inc(d_hn, 1)
                g, s, live = at(j, u, "h")
                if live:
                    products(g, u, row, 1, p_k, 2)
                g, s, live = at(j, u, "pT")
                if live:
                    wait(dve, p_pT, 2 * g + 2)
                    dve.tensor_copy(prT[:, 1, :, :], ps[:, 5, :].rearrange("p (c n) -> p c n", c=HP)).then_inc(d_pT, 1)
                g, s, live = at(j, u, "hnT")
                if live:
                    wait(dve, a_hnTh, g + 1)
                    dve.tensor_tensor(hnTl[:, s, :], ps[:, 0, 2 * P:3 * P], hnTh[:, s, :].bitcast(F32), ALU.subtract).then_inc(d_hnTl, 1)
                g, s, live = at(j, u, "h")
                if live:
                    products(g, u, row, 0, p_q, 1)
                g, s, live = at(j, u, "pT")
                if live:
                    wait(dve, p_pv, 2 * g + 1)
                    dve.reciprocal(ro[:, s % 2, 0, :], sums_of(0)[:, :, DH]).then_inc(d_ro, 1)
                g, s, live = at(j, u, "pT")
                if live:
                    wait(dve, p_pv, 2 * g + 2)
                    dve.reciprocal(ro[:, s % 2, 1, :], sums_of(1)[:, :, DH]).then_inc(d_ro, 1)
                g, s, live = at(j, u, "pT")
                if live:
                    wait(dve, d_ro, 2 * g + 1)
                    dve.tensor_tensor(on[:, :, 0, :], sums_of(0)[:, :, 0:DH],
                                      ro[:, s % 2, 0, :].unsqueeze(2).to_broadcast([P, HP, DH]), ALU.mult).then_inc(d_on, 1)
                g, s, live = at(j, u, "pT")
                if live:
                    wait(dve, d_ro, 2 * g + 2)
                    dve.tensor_tensor(on[:, :, 1, :], sums_of(1)[:, :, 0:DH],
                                      ro[:, s % 2, 1, :].unsqueeze(2).to_broadcast([P, HP, DH]), ALU.mult).then_inc(d_on, 1)
                g, s, live = at(j, u, "oT")
                if live:
                    wait(dve, m_h2[s], 3 * 16 * (g // R + 1))
                    dve.bn_stats(st2[:, s % 2, :], h2_r[:, s, :]).then_inc(d_st2, 1)
                g, s, live = at(j, u, "h")
                if live:
                    wait(dve, a_sq, 2 * g + 2)
                    dve.tensor_reduce(out=n2[:, s, :], in_=sq[:].rearrange("p a (h c) -> p (a h) c", h=H), axis=AX.X,
                                      op=ALU.add).then_inc(d_ns, 1)
                g, s, live = at(j, u, "uT")
                if live:
                    wait(dve, p_w2, g + 1)
                    dve.tensor_tensor(tile_of(xs, w2_slot), ps[:, 0, 3 * P:4 * P], tile_of(x2s, w2_slot2), ALU.add).then_inc(d_x, 1)
                g, s, live = at(j, u, "h")
                if live:
                    wait(dve, d_ns, g + 1)
                    dve.tensor_scalar(n2[:, s, :], n2[:, s, :], NORM_FLOOR2, -0.5, ALU.max, ALU.mult).then_inc(d_nc, 1)
                g, s, live = at(j, u, "oT")
                if live:
                    wait(dve, d_st2, g + 1)
                    dve.memset(gap[:, :], 0.0)
                    dve.bn_aggr(mv2[:, s, :], st2[:, s % 2, :]).then_inc(d_mv2, 1)
                g, s, live = at(j, u, "h")
                if live:
                    wait(dve, d_nc, g + 1)
                    seed(rn[:, s, :], n2[:, s, :]).then_inc(d_n2, 1)
                g, s, live = at(j, u, "oT")
                if live:
                    wait(dve, d_mv2, g + 1)
                    dve.tensor_scalar(mm[:, u, 2 * H:2 * H + 1], mv2[:, s, 1:2], EPS, -0.5, ALU.add, ALU.mult).then_inc(d_eps2, 1)
                g, s, live = at(j, u, "oT")
                if live:
                    wait(dve, d_eps2, g + 1)
                    seed(yy[:, u, 2 * H:2 * H + 1], mm[:, u, 2 * H:2 * H + 1]).then_inc(d_var2, 1)
                g, s, live = at(j, u, "u")
                if live and s % 2 == 0:
                    wait(dve, a_ge, g // 2 + 1)
                    wait(dve, d_a, g + 2)
                    dve.tensor_tensor(fu[:, s:s + 2, 0:HE], fa[:, s:s + 2, :], fg[:, s:s + 2, :], ALU.mult).then_inc(d_u, 1)

                if isinstance(j, int) and j >= G:
                    last = j - SKEW["uT"] - T
                    outs = [(last, last + 1)]
                    if j == G:
                        outs = [(0, T // 2)] + [(t, t + 1) for t in range(T // 2, last + 1)]
                    for a, b in outs:
                        if a < b:
                            wait(dve, d_x, 2 * T + b)
                            base = slot(a)
                            dve.tensor_tensor(x1[:, a:b, :], x1[:, a:b, :], xs[:, base:base + b - a, :], ALU.add).then_inc(s_y, 1)

            stream(dve, step, hand_over(dve, astep, step))

        @block.tensor
        def _(pe):
            pe.wait_ge(s_eye, 16 * NLOAD_EYE)
            pe.wait_ge(s_wa, 16 * NLOAD_WA)
            for a in range(2):
                pe.matmul(ps[:, 0, a * P:(a + 1) * P], wa[:, a, :], turn[:, :], start=True, stop=True)
                pe.matmul(ps[:, 0, 3 * P + a:3 * P + a + 1], turn[:, :], ba[:, a:a + 1], start=True, stop=True)
            pe.transpose(ps[:, 0, 2 * P:3 * P], wa[:, 2, :], eye[:, :]).then_inc(s_wpe, 1)
            pe.wait_ge(s_wprep_act, 1)

            for n in range(NG + 1):
                if n < NG:
                    pe.wait_ge(s_xn, n + 1)
                    wait(pe, s_axTs, n - 1)
                    for k in range(GT):
                        last = pe.transpose(ps[:, 2 + n % 2, k * P:(k + 1) * P], xn[:, n % 2, k * D:(k + 1) * D], eye[:, :])
                    last.then_inc(s_axT, 1)
                if n >= 1:
                    g = n - 1
                    k_bank, q_bank, v_bank = group_banks(g)
                    pe.wait_ge(s_axTs, g + 1)
                    wait(pe, s_ak32, g - 1)
                    pe.matmul(ps[:, k_bank, :], waT[:, 1, :], xnT[:, g % 2, :], start=True, stop=True).then_inc(s_apk, 1)
                    wait(pe, s_aq, g - 1)
                    pe.matmul(ps[:, q_bank, :], waT[:, 0, :], xnT[:, g % 2, :], start=True, stop=True).then_inc(s_apq, 1)
                    wait(pe, s_ava, g - 1)
                    for k in range(GT):
                        last = pe.matmul(ps[:, v_bank, k * P:(k + 1) * P], xnT[:, g % 2, k * P:(k + 1) * P], waT[:, 2, :],
                                         start=True, stop=True)
                    last.then_inc(s_apv_own, 1)

            pe.wait_ge(s_ak, NG)

            def astep(j, u):
                if has(j, 1):
                    g, s = j - 1, (u - 1) % R
                    wait(pe, s_aql, g + 1)
                    wait(pe, s_aex, g - 1)
                    for n in range(2):
                        cols = bass.ds((g // TB) * N + n * 512, 512)
                        last = split3(pe, ps[:, 2 * (s % 2) + n, :], qh[:, s, :], ql[:, s, :],
                                      kTh[:, :, :].rearrange("p b n -> p (b n)")[:, cols],
                                      kTl[:, :, :].rearrange("p b n -> p (b n)")[:, cols])
                    last.then_inc(s_asc, 1)
                if isinstance(j, int) and j == 1:
                    pe.wait_ge(s_wl, 16 * NLOAD_WL)
                    pe.wait_ge(s_ava, NG)
                    for l in range(DEPTH):
                        for a in range(2):
                            last = pe.matmul(ps[0:2, 4 + 2 * l + a, 0:HE], lnb[:, l, :], w1[:, l, a, :], start=True, stop=True)
                    last.then_inc(s_wpe, 1)
                if has(j, 2):
                    g, s = j - 2, (u - 2) % 2
                    if isinstance(j, int) and j == 2:
                        pe.wait_ge(s_wprep, 1)
                    wait(pe, s_aex, g + 1)
                    wait(pe, s_apTa, g)
                    for c in range(TB):
                        last = pe.transpose(ps[:, 4 + c // 4, (c % 4) * P:(c % 4 + 1) * P], pa[:, s, c * P:(c + 1) * P], eye[:, :])
                    last.then_inc(s_apT, 1)
                if has(j, 3):
                    g, s = j - 3, (u - 3) % 2
                    wait(pe, s_apTa, g + 1)
                    wait(pe, s_ax1, g - 1)
                    for c in range(TB):
                        last = pe.matmul(ps[:, 6 + s, 0:P], paT[:, s, c * P:(c + 1) * P],
                                         va[:, bass.ds((g // TB) * TB + c, 1), :].rearrange("p a n -> p (a n)"),
                                         start=(c == 0), stop=(c == TB - 1))
                    last.then_inc(s_apv, 1)

            attend(pe, astep)
            pe.wait_ge(s_gprep, DEPTH + 1)
            pe.wait_ge(s_xtab, 1)
            pe.wait_ge(s_wprep_act, 6)
            pe.wait_ge(s_ready, 3)
            pe.wait_ge(s_wprep, 3)

            def scores(g, s, b, first):
                wait(pe, a_qT, g + 1)
                wait(pe, a_kT, g + 1)
                wait(pe, a_exp, 2 * g - 1 + b)
                pe.matmul(ps[:, 6 + b, :], eye16[:, :], mask[:, bass.ds(first, 1), :].rearrange("p o n -> p (o n)"),
                          start=True, stop=False, skip_group_check=True)
                rows = slice(DH * b, DH * (b + 1))
                for c in range(HP):
                    for w in range(2):
                        last = pe.matmul(ps[W * w:W * (w + 1), 6 + b, c * P:(c + 1) * P],
                                         qT[rows, s % 2, c, W * w:W * (w + 1)],
                                         kT[rows, c, s * P + W * w:s * P + W * w + 2 * W],
                                         start=False, stop=True, skip_group_check=True)
                last.then_inc(p_sc, 1)

            def values(s, b):
                for c in range(HP):
                    h = 2 * c + b
                    for w, v in enumerate((v_back, v_own)):
                        last = pe.matmul(ps[W * w:W * (w + 1), 4 + b, c * (DH + 1):(c + 1) * (DH + 1)],
                                         prT[:, b, c, W * w:W * (w + 1)], v[:, s, h, :], start=True, stop=True)
                last.then_inc(p_pv, 1)

            def step(j, u):
                if isinstance(j, int) and j == 0:
                    pe.wait_ge(s_aex, T)
                if isinstance(j, int) and j == 2:
                    pe.wait_ge(s_apTa, T)
                    pe.wait_ge(s_ax1, T)
                l_qkv, l_wo, l_w1, l_w2 = (ahead(pe, "l_" + stage, layer(at(j, u, stage)[0]), DEPTH - 1) for stage in ("h", "oT", "w1", "uT"))
                first = ahead(pe, "first", (at(j, u, "qkT")[0] % TB + TB - 1) // TB, 1)
                g, s, live = at(j, u, "qkT")
                if live:
                    r = s % 2
                    wait(pe, g_q, g + 1)
                    wait(pe, d_on, 2 * through(j - 1, "pT") - 1)
                    for c in range(HP):
                        last = pe.transpose(ps[:, 4, c * P:(c + 1) * P], qk[:, r, 0, c * P:(c + 1) * P], eye[:, :])
                    last.then_inc(p_qT, 1)
                g, s, live = at(j, u, "qkT")
                if live:
                    r = s % 2
                    wait(pe, g_k, g + 1)
                    wait(pe, d_on, 2 * through(j - 1, "pT"))
                    for c in range(HP):
                        last = pe.transpose(ps[:, 5, c * P:(c + 1) * P], qk[:, r, 1, c * P:(c + 1) * P], eye[:, :])
                    last.then_inc(p_kT, 1)
                g, s, live = at(j, u, "w1")
                if live:
                    wait(pe, d_hnTl, g + 1)
                    wait(pe, d_t, 2 * through(j - 1, "h"))
                    wait(pe, a_sq, 2 * through(j - 1, "h"))
                    for a in range(2):
                        o = ps[:, 1 + a, 0:HE]
                        pe.matmul(o, ones2[:, :], b1_hl[:, bass.ds(l_w1, 1), a, :].rearrange("p o n -> p (o n)"), start=True, stop=False)
                        last = split3(pe, o, hnTh[:, s, :], hnTl[:, s, :],
                                      w1_h[:, bass.ds(l_w1, 1), a, :].rearrange("p o n -> p (o n)"),
                                      w1_l[:, bass.ds(l_w1, 1), a, :].rearrange("p o n -> p (o n)"), start=False)
                    last.then_inc(p_w1, 1)
                g, s, live = at(j, u, "oT")
                if live:
                    wait(pe, d_on, 2 * g + 2)
                    wait(pe, a_v, through(j - 1, "h"))
                    for c in range(4):
                        last = pe.transpose(ps[:, 3, c * P:(c + 1) * P],
                                            on[:, c, :, :].rearrange("p b n -> p (b n)"), eye[:, :])
                    last.then_inc(p_oT, 1)
                g, s, live = at(j, u, "h")
                if live:
                    wait(pe, m_h[s], 3 * 16 * (g // R + 1))
                    wait(pe, d_x, T + through(j - 1, "uT"))
                    pe.transpose(ps[:, 0, 0:P], h_r[:, s, :], eye[:, :]).then_inc(p_hT, 1)
                g, s, live = at(j, u, "qkT")
                if live:
                    scores(g, s, 0, first)
                g, s, live = at(j, u, "qkT")
                if live:
                    scores(g, s, 1, first)
                g, s, live = at(j, u, "uT")
                if live:
                    wait(pe, d_u, g // 2 + 1)
                    wait(pe, d_a, through(j, "w1"))
                    for c in range(HC):
                        last = pe.transpose(ps[:, 1, c * P:(c + 1) * P], fu[:, s, c * P:(c + 1) * P], eye[:, :])
                    last.then_inc(p_uT, 1)
                g, s, live = at(j, u, "oT")
                if live:
                    wait(pe, a_oT, g + 1)
                    wait(pe, d_hTl, through(j, "h"))
                    if isinstance(j, int):
                        wait(pe, d_x, T + through(j - 1, "uT"))
                    for c in range(4):
                        last = pe.matmul(ps[:, 0, P:2 * P], oT[:, s % 2, c, :],
                                         wo[:, bass.ds(l_wo, 1), c, :].rearrange("p o n -> p (o n)"), start=c == 0, stop=c == 3)
                    last.then_inc(p_wo, 1)
                g, s, live = at(j, u, "h")
                if live:
                    wait(pe, d_hTl, g + 1)
                    wait(pe, a_g, through(j, "w1"))
                    split3(pe, ps[:, 2, :], hTh[:, s, :], hTl[:, s, :],
                           wqkv_h[:, bass.ds(l_qkv, 1), INNER:2 * INNER].rearrange("p o n -> p (o n)"),
                           wqkv_l[:, bass.ds(l_qkv, 1), INNER:2 * INNER].rearrange("p o n -> p (o n)")).then_inc(p_k, 1)
                g, s, live = at(j, u, "pT")
                if live:
                    wait(pe, a_exp, 2 * g + 1)
                    wait(pe, a_qT, through(j, "qkT"))
                    for c in range(HP):
                        last = pe.transpose(ps[:, 4, c * P:(c + 1) * P], pr[:, s % 2, 0, c, :], eye[:, :])
                    last.then_inc(p_pT, 1)
                g, s, live = at(j, u, "pT")
                if live:
                    wait(pe, a_exp, 2 * g + 2)
                    wait(pe, a_kT, through(j, "qkT"))
                    for c in range(HP):
                        last = pe.transpose(ps[:, 5, c * P:(c + 1) * P], pr[:, s % 2, 1, c, :], eye[:, :])
                    last.then_inc(p_pT, 1)
                g, s, live = at(j, u, "hnT")
                if live:
                    wait(pe, d_hn, g + 1)
                    wait(pe, d_x2, through(j, "oT"))
                    pe.transpose(ps[:, 0, 2 * P:3 * P], hn[:, s % 2, :], eye[:, :]).then_inc(p_hnT, 1)
                g, s, live = at(j, u, "h")
                if live:
                    wait(pe, d_hTl, g + 1)
                    wait(pe, d_a, through(j, "w1"))
                    wait(pe, a_uT, through(j, "uT"))
                    split3(pe, ps[:, 1, :], hTh[:, s, :], hTl[:, s, :],
                           wqkv_h[:, bass.ds(l_qkv, 1), 0:INNER].rearrange("p o n -> p (o n)"),
                           wqkv_l[:, bass.ds(l_qkv, 1), 0:INNER].rearrange("p o n -> p (o n)")).then_inc(p_q, 1)
                g, s, live = at(j, u, "h")
                if live:
                    wait(pe, d_hTl, g + 1)
                    wait(pe, a_oT, through(j, "oT"))
                    split3(pe, ps[:, 3, :], hTh[:, s, :], hTl[:, s, :],
                           wqkv_h[:, bass.ds(l_qkv, 1), 2 * INNER:3 * INNER].rearrange("p o n -> p (o n)"),
                           wqkv_l[:, bass.ds(l_qkv, 1), 2 * INNER:3 * INNER].rearrange("p o n -> p (o n)")).then_inc(p_v, 1)
                g, s, live = at(j, u, "pT")
                if live:
                    wait(pe, a_pT, g + 1)
                    wait(pe, m_v[s], 2 * 16 * (g // R + 1))
                    values(s, 0)
                g, s, live = at(j, u, "pT")
                if live:
                    wait(pe, d_pT, g + 1)
                    values(s, 1)
                g, s, live = at(j, u, "uT")
                if live:
                    wait(pe, a_uT, g + 1)
                    wait(pe, d_hnTl, through(j, "hnT"))
                    wait(pe, d_x, T + g)
                    pe.matmul(ps[:, 0, 3 * P:4 * P], ones2[:, :], b2_hl[:, bass.ds(l_w2, 1), :].rearrange("p o n -> p (o n)"),
                              start=True, stop=False)
                    for c in range(HC):
                        last = pe.matmul(ps[:, 0, 3 * P:4 * P], fuT[:, s % 2, c, :],
                                         w2[:, bass.ds(l_w2, 1), c, :].rearrange("p o n -> p (o n)"), start=False, stop=c == HC - 1)
                    last.then_inc(p_w2, 1)

            stream(pe, step, hand_over(pe, astep, step))


_LOADS = {"x": "L0_attn_hidden_states", "Wq": "L0_attn_Wq", "bq": "L0_attn_bq", "Wk": "L0_attn_Wk", "bk": "L0_attn_bk",
          "Wv": "L0_attn_Wv", "bv": "L0_attn_bv", "wqkv": "L0_ffn_wqkv", "wo": "L0_ffn_wo", "ln_g": "L0_ffn_ln_g",
          "ln_b": "L0_ffn_ln_b", "w1": "L0_ffn_w1", "b1": "L0_ffn_b1", "w2": "L0_ffn_w2", "b2": "L0_ffn_b2"}


def kernel(**inputs):
    import concourse.bacc as bacc
    from concourse.bass_utils import run_bass_kernel_spmd

    nc = bacc.Bacc("TRN2", target_bir_lowering=False, num_devices=1)
    arrays = {name: np.ascontiguousarray(inputs[key]) for name, key in _LOADS.items()}
    arrays["scales"] = np.concatenate([np.asarray(inputs["L0_ffn_q_scale"]).ravel(), np.asarray(inputs["L0_ffn_k_scale"]).ravel()])
    arrays["ln_g"] = np.ascontiguousarray(arrays["ln_g"].T)
    arrays["ln_b"] = np.ascontiguousarray(np.stack([arrays["ln_b"].T] * 2, axis=-1))
    arrays.update(constants())
    dram = {name: nc.dram_tensor("in_" + name, a.shape, mybir.dt.from_np(a.dtype), kind="ExternalInput").ap()
            for name, a in arrays.items()}
    out = nc.dram_tensor("out", (B, N, D), F32, kind="ExternalOutput").ap()
    build(nc, dram, out)
    return run_bass_kernel_spmd(nc, [{"in_" + n: a for n, a in arrays.items()}], core_ids=[0]).results[0]["out"]
```
